# Optimizing a Trainium2 kernel written in Bass

```python
import numpy as np
import jax
import jax.numpy as jnp

def _softmax(x, axis=-1):
    return jax.nn.softmax(x, axis=axis)

def _gelu(x):
    return jax.nn.gelu(x, approximate=True)

def _silu(x):
    return jax.nn.silu(x)

def _sigmoid(x):
    return jax.nn.sigmoid(x)

def _layernorm(x, axis=-1, eps=1e-05):
    m = jnp.mean(x, axis=axis, keepdims=True)
    v = jnp.var(x, axis=axis, keepdims=True)
    return (x - m) / jnp.sqrt(v + eps)

def _scatter_add(tgt, idx, src, axis=0):
    return tgt.at[idx].add(src)

def _segment_sum(src, seg, n):
    return jax.ops.segment_sum(src, seg, n)
kernel_name = 'mk_xattn_ffn_d1_seqx_r4_77f853'

def setup_inputs(seed: int=0):
    np.random.seed(seed)
    _w = jnp.asarray

    def _rec_inputs():
        import jax
        import jax.numpy as jnp
        _rk = jax.random.key(seed)
        x = 7.22e-05 + 1 * jax.random.normal(jax.random.fold_in(_rk, 1), (8, 256, 256), jnp.float32)
        _lenS = 256 - jax.random.randint(jax.random.fold_in(_rk, 7), (8,), 0, max(1, 256 // 4) + 1, jnp.int32)
        _lenS2 = 256 - jax.random.randint(jax.random.fold_in(_rk, 8), (8,), 0, max(1, 256 // 4) + 1, jnp.int32)
        _ctx_1024P = jax.random.normal(jax.random.fold_in(_rk, 11), (8, 16, 256), jnp.float32)
        _ctx_1024c = jax.random.dirichlet(jax.random.fold_in(_rk, 511), 0.3 * jnp.ones((16,), jnp.float32), (8, 256))
        _ctx_1024t = jnp.einsum('bsk,bkd->bsd', _ctx_1024c, _ctx_1024P)
        _ctx_1024t = _ctx_1024t * jax.lax.rsqrt(jnp.mean(jnp.square(_ctx_1024t)) + 1e-12) * 0.953939
        ctx_1024 = 4.13588e-05 + 0.999923 * (_ctx_1024t + 0.3 * jax.random.normal(jax.random.fold_in(_rk, 611), (8, 256, 256), jnp.float32))
        _validS = jnp.arange(256)[None, :] < _lenS[:, None]
        _validS2 = jnp.arange(256)[None, :] < _lenS2[:, None]
        _causal = jnp.tril(jnp.ones((256, 256), dtype=bool))
        mask_BxS2_ik1 = jnp.where(jnp.broadcast_to(_validS2[:, :], (8, 256)), 1, 0).astype(jnp.int32)
        return (x, ctx_1024, mask_BxS2_ik1)
    x, ctx_1024, mask_BxS2_ik1 = _rec_inputs()

    def _L0_xattn_setup():
        import jax, jax.numpy as jnp
        import numpy as np
        import math
        B, T, EMB = (4, 512, 256)
        PAD_TAIL = 64
        key = jax.random.key(seed)
        kq, kk, kv = jax.random.split(key, 3)
        query = jax.random.normal(kq, (B, T, EMB), dtype=jnp.float32)
        k = jax.random.normal(kk, (B, T, EMB), dtype=jnp.float32)
        value = jax.random.normal(kv, (B, T, EMB), dtype=jnp.float32)
        attention_mask = jnp.concatenate([jnp.ones((B, T - PAD_TAIL), dtype=jnp.int32), jnp.zeros((B, PAD_TAIL), dtype=jnp.int32)], axis=1)
        return {'query': query, 'key': k, 'value': value, 'attention_mask': attention_mask}
    _L0_xattn_all = _L0_xattn_setup()
    _L0_xattn_in = {k: v for k, v in _L0_xattn_all.items() if k in ()}
    del _L0_xattn_all

    def _L0_ffn_setup():
        import jax, jax.numpy as jnp
        import numpy as np
        D_IN, D_HID = (256, 1024)

        def _ternary(key, shape):
            return jax.random.randint(key, shape, -1, 2).astype(jnp.float32)

        def _tlin(x, w, s):
            return jnp.einsum('bsi,oi->bso', x, w) * s
        key = jax.random.key(seed)
        ks = jax.random.split(key, 12)
        inv = lambda fan: 1.0 / np.sqrt(fan).astype(np.float32)
        return {'x': jax.random.normal(ks[0], (4, 512, D_IN), dtype=jnp.float32), 'w1_w': _ternary(ks[1], (D_HID, D_IN)), 'w1_s': jax.random.uniform(ks[2], (D_HID,), dtype=jnp.float32) * inv(D_IN), 'w2_w': _ternary(ks[3], (D_HID, D_IN)), 'w2_s': jax.random.uniform(ks[4], (D_HID,), dtype=jnp.float32) * inv(D_IN), 'h1_w': _ternary(ks[5], (D_HID, D_HID)), 'h1_s': jax.random.uniform(ks[6], (D_HID,), dtype=jnp.float32) * inv(D_HID), 'h2_w': _ternary(ks[7], (D_HID, D_HID)), 'h2_s': jax.random.uniform(ks[8], (D_HID,), dtype=jnp.float32) * inv(D_HID), 'w3_w': _ternary(ks[9], (D_IN, D_HID)), 'w3_s': jax.random.uniform(ks[10], (D_IN,), dtype=jnp.float32) * inv(D_HID)}
    _L0_ffn_all = _L0_ffn_setup()
    _L0_ffn_in = {k: v for k, v in _L0_ffn_all.items() if k in ('w1_w', 'w1_s', 'w2_w', 'w2_s', 'h1_w', 'h1_s', 'h2_w', 'h2_s', 'w3_w', 'w3_s')}
    del _L0_ffn_all
    return {'x': x, 'ctx_1024': ctx_1024, 'mask_BxS2_ik1': mask_BxS2_ik1, 'L0_ffn_w1_w': _L0_ffn_in['w1_w'], 'L0_ffn_w1_s': _L0_ffn_in['w1_s'], 'L0_ffn_w2_w': _L0_ffn_in['w2_w'], 'L0_ffn_w2_s': _L0_ffn_in['w2_s'], 'L0_ffn_h1_w': _L0_ffn_in['h1_w'], 'L0_ffn_h1_s': _L0_ffn_in['h1_s'], 'L0_ffn_h2_w': _L0_ffn_in['h2_w'], 'L0_ffn_h2_s': _L0_ffn_in['h2_s'], 'L0_ffn_w3_w': _L0_ffn_in['w3_w'], 'L0_ffn_w3_s': _L0_ffn_in['w3_s']}

def reference(x, ctx_1024, mask_BxS2_ik1, L0_ffn_w1_w, L0_ffn_w1_s, L0_ffn_w2_w, L0_ffn_w2_s, L0_ffn_h1_w, L0_ffn_h1_s, L0_ffn_h2_w, L0_ffn_h2_s, L0_ffn_w3_w, L0_ffn_w3_s):
    import jax
    import jax.numpy as jnp

    def _L0_xattn_ref(query, key, value, attention_mask):
        import jax, jax.numpy as jnp
        import numpy as np
        import math
        B, T, EMB = (4, 512, 256)
        PAD_TAIL = 64
        Bq, Tq, emb = query.shape
        Tk = key.shape[1]
        scale = 1.0 / math.sqrt(emb)
        scores = jnp.einsum('bqd,bkd->bqk', query, key) * scale
        neg_inf = jnp.float32(-jnp.inf)
        if Tq == Tk:
            causal = jnp.triu(jnp.ones((Tq, Tk), dtype=bool), k=1)
            scores = jnp.where(causal[None, :, :], neg_inf, scores)
        key_pad = (attention_mask == 0)[:, None, :]
        scores = jnp.where(key_pad, neg_inf, scores)
        attn = jax.nn.softmax(scores, axis=-1)
        out = jnp.einsum('bqk,bkd->bqd', attn, value)
        return out

    def _L0_ffn_ref(x, w1_w, w1_s, w2_w, w2_s, h1_w, h1_s, h2_w, h2_s, w3_w, w3_s):
        import jax, jax.numpy as jnp
        import numpy as np
        D_IN, D_HID = (256, 1024)

        def _ternary(key, shape):
            return jax.random.randint(key, shape, -1, 2).astype(jnp.float32)

        def _tlin(x, w, s):
            return jnp.einsum('bsi,oi->bso', x, w) * s
        h = jax.nn.silu(_tlin(x, w1_w, w1_s)) * _tlin(x, w2_w, w2_s)
        h = jax.nn.gelu(_tlin(h, h1_w, h1_s), approximate=False)
        h = jax.nn.gelu(_tlin(h, h2_w, h2_s), approximate=False)
        return _tlin(h, w3_w, w3_s)
    x = x + _L0_xattn_ref(_layernorm(x, axis=-1), ctx_1024, ctx_1024, mask_BxS2_ik1)
    x = x + _L0_ffn_ref(_layernorm(x, axis=-1), L0_ffn_w1_w, L0_ffn_w1_s, L0_ffn_w2_w, L0_ffn_w2_s, L0_ffn_h1_w, L0_ffn_h1_s, L0_ffn_h2_w, L0_ffn_h2_s, L0_ffn_w3_w, L0_ffn_w3_s)
    return x

_drawn_inputs = setup_inputs


def setup_inputs(seed=0):
    import zlib

    import numpy as np

    out = dict(_drawn_inputs(seed))
    spreads = {}
    factors = {}
    for name, (base, spread) in spreads.items():
        noise = np.random.default_rng([zlib.crc32(name.encode()), seed]).standard_normal(out[name].shape)
        drawn = base * np.exp(spread * noise) if base else spread * noise
        out[name] = jnp.asarray(drawn.astype(out[name].dtype))
    for name, factor in factors.items():
        out[name] = (out[name] * factor).astype(out[name].dtype)
    return out
```

```python
from contextlib import ExitStack

import concourse.bass as bass
from concourse import mybir

F32 = mybir.dt.float32
F32R = mybir.dt.float32r
BF16 = mybir.dt.bfloat16
I32 = mybir.dt.int32
U16 = mybir.dt.uint16
ALU = mybir.AluOpType
ACT = mybir.ActivationFunctionType
RADD = bass.bass_isa.ReduceOp.add

P = 128
BATCH, SEQ, EMB, HID = 8, 256, 256, 1024
PAIR = 2
TOK = PAIR * SEQ
TILES = BATCH // PAIR
ROWS = TOK // P
EC = EMB // P
HC = HID // P
KEYS = P + SEQ
EPS = 1e-5
SCALE = float(EMB) ** -0.5
MASKED = -1.5e38
FLOOR = -1.0e37

PIECE = 1024
GU_P = 2 * EC * HID // PIECE
H_P = HC * HID // PIECE
DOWN_P = HC * EMB // PIECE
PIECES = GU_P + 2 * H_P + DOWN_P
SEGMENTS = [(0, GU_P), (GU_P, H_P // 2), (GU_P + H_P // 2, H_P // 2),
            (GU_P + H_P, H_P // 2), (GU_P + H_P + H_P // 2, H_P // 2), (GU_P + 2 * H_P, DOWN_P)]
GATE_UP, HID1A, HID1B, HID2A, HID2B, DOWN = range(6)
RING = 6
CH = 3 * HC


def xattn_ffn(nc, x, ctx_rows_d, ctx_cols_d, mask_d, weights_d, scales_d, down_scale_d, out):
    staged_d = nc.dram_tensor("weights_staged", [PIECES, P, PIECE], F32).ap()
    x_v = x.rearrange("(t r p) d -> t p r d", p=P, r=ROWS)
    ctx_v = ctx_rows_d.rearrange("(t r p) d -> t p r d", p=P, r=ROWS)
    out_v = out.rearrange("(t r p) d -> t p r d", p=P, r=ROWS)

    stack = ExitStack()
    with stack:
        def sb(name, shape, dt=F32):
            return stack.enter_context(nc.sbuf_tensor(name, shape, dt))

        def sem(name):
            return stack.enter_context(nc.semaphore(name))

        weights = sb("weights", [P, PIECES, PIECE], F32R)
        h_hi = [sb(f"h_hi{n}", [P, HC, TOK], F32R) for n in range(2)]
        h_lo = [sb(f"h_lo{n}", [P, HC, TOK], F32R) for n in range(2)]
        xn_hi = sb("xn_hi", [P, EC, TOK], F32R)
        xn_lo = sb("xn_lo", [P, EC, TOK], F32R)
        x_in = sb("x_in", [P, ROWS, EMB])
        x_attn = sb("x_attn", [P, ROWS, EMB])
        residual = sb("residual", [P, ROWS, EMB])
        ctx_rows = sb("ctx_rows", [P, ROWS, EMB])
        ctx_cols = sb("ctx_cols", [P, EC, TOK])
        mask = sb("mask", [P, PAIR, KEYS])
        work = sb("work", [P, ROWS * EMB])
        turned = sb("turned", [P, EC * TOK])
        gate = sb("gate", [P, 2, TOK])
        act32 = sb("act32", [P, 3, TOK])
        down_scale = sb("down_scale", [P, EMB])
        scales = sb("scales", [P, 4, HC])
        ident = sb("ident", [P, P])
        tri = sb("tri", [P, P])
        test_out = sb("test_out", [P, PIECE], BF16)
        low_sums = sb("low_sums", [P, PIECES])
        seg_sums = sb("seg_sums", [P, 6])
        seg_flags = sb("seg_flags", [P, 6])
        stats = sb("stats", [P, ROWS, 6])
        mean_var = sb("mean_var", [P, ROWS, 2])
        var_eps = sb("var_eps", [P, ROWS])
        rstd = sb("rstd", [P, ROWS])
        minus_half = sb("minus_half", [P, ROWS])
        row_max = sb("row_max", [P, ROWS])
        neg_max = sb("neg_max", [P, ROWS])
        row_sum = sb("row_sum", [P, ROWS])
        inv_sum = sb("inv_sum", [P, ROWS])

        xn = work[:].rearrange("p (r d) -> p r d", r=ROWS)
        probs = work[:, 0:PAIR * KEYS].rearrange("p (b k) -> p b k", b=PAIR)
        q_cols = turned[:].rearrange("p (c t) -> p c t", c=EC)
        probs_t = turned[:, 0:PAIR * KEYS].rearrange("p (b k) -> p b k", b=PAIR)
        gate_scale, up_scale, h1_scale, h2_scale = (scales[:, n] for n in range(4))

        att = [stack.enter_context(nc.psum_tensor(f"att{n}", [P, 512], F32)) for n in range(2)]
        ring = [stack.enter_context(nc.psum_tensor(f"ring{n}", [P, 512], F32)) for n in range(RING)]

        staged = [sem(f"staged{n}") for n in range(PIECES)]
        loaded = [sem(f"loaded{n}") for n in range(PIECES)]
        consts_in = sem("consts_in")
        x_loaded = sem("x_loaded")
        ctx_loaded = sem("ctx_loaded")
        mask_loaded = sem("mask_loaded")
        out_stored = sem("out_stored")
        ident_made = sem("ident_made")
        tri_made = sem("tri_made")
        pool_step = sem("pool_step")
        mask_made = sem("mask_made")
        rstd_ready = sem("rstd_ready")
        flag_ready = sem("flag_ready")
        low_summed = sem("low_summed")
        q_evacuated = sem("q_evacuated")
        probs_ready = sem("probs_ready")
        xn_hi_ready = sem("xn_hi_ready")
        residual_set = sem("residual_set")
        gate_done = sem("gate_done")
        hi_done = sem("hi_done")
        gelu_done = sem("gelu_done")
        stats_step = sem("stats_step")
        moments = sem("moments")
        xn_ready = sem("xn_ready")
        maxed = sem("maxed")
        neg_ready = sem("neg_ready")
        inv_ready = sem("inv_ready")
        probs_evac = sem("probs_evac")
        x_attn_done = sem("x_attn_done")
        xn_split = sem("xn_split")
        gated = sem("gated")
        hi_made = sem("hi_made")
        split = sem("split")
        down_free = sem("down_free")
        result_done = sem("result_done")
        q_turned = sem("q_turned")
        scores_done = sem("scores_done")
        probs_turned = sem("probs_turned")
        attended = sem("attended")
        xn_turned = sem("xn_turned")
        gate_mm = sem("gate_mm")
        up_mm = sem("up_mm")
        hid_mm = sem("hid_mm")
        down_mm = sem("down_mm")

        def half(b, q):
            return (b, slice(0, P)) if q == 0 else (b, slice(P, KEYS))

        block = stack.enter_context(nc.Block())

        @block.sync
        def _(sp):
            def load_context(t):
                sp.dma_start(ctx_cols[:], ctx_cols_d[t]).then_inc(ctx_loaded, 16)
                sp.dma_start(ctx_rows[:], ctx_v[t]).then_inc(ctx_loaded, 16)

            def load_mask(t):
                sp.dma_start(mask[:].bitcast(I32), mask_d[t].partition_broadcast(P)).then_inc(mask_loaded, 16)

            def load_next(t):
                sp.wait_ge(x_attn_done, ROWS * t)
                sp.dma_start(x_in[:], x_v[t]).then_inc(x_loaded, 16)
                load_context(t)
                sp.wait_ge(maxed, ROWS * t)
                load_mask(t)

            def stage(n):
                sp.dma_start(staged_d[n], weights_d[n]).then_inc(staged[n], 16)

            def load_piece(n):
                sp.wait_ge(staged[n], 16)
                sp.dma_start(weights[:, n].bitcast(F32), staged_d[n]).then_inc(loaded[n], 16)

            def store(t):
                for r in range(ROWS):
                    sp.wait_ge(result_done, ROWS * t + r + 1)
                    sp.dma_start(out_v[t][:, r], residual[:, r]).then_inc(out_stored, 16)

            ahead = 3
            sp.dma_start(x_in[:], x_v[0]).then_inc(x_loaded, 16)
            for n in range(ahead):
                stage(n)
                if n == 0:
                    sp.dma_start(scales[:], scales_d).then_inc(consts_in, 16)
                    sp.dma_start(down_scale[:], down_scale_d.partition_broadcast(P)).then_inc(consts_in, 16)
                    load_context(0)
                    load_mask(0)
            for n in range(PIECES):
                if n + ahead < PIECES:
                    stage(n + ahead)
                load_piece(n)
                if n == GU_P + H_P // 2 - 1:
                    load_next(1)
            with sp.Fori(0, TILES - 2) as t:
                load_next(t + 2)
                store(t)
            for t in range(TILES - 2, TILES):
                store(t)
            sp.wait_ge(out_stored, 16 * ROWS * TILES)

        @block.gpsimd
        def _(pool):
            steps = [0]

            def chain(ins):
                ins.then_inc(pool_step, 1)
                steps[0] += 1
                pool.wait_ge(pool_step, steps[0])

            chain(nc.gpsimd.memset(ident[:], 0.0))
            nc.gpsimd.affine_select(out=ident[:], in_=ident[:], compare_op=ALU.not_equal, fill=1.0, base=0,
                                    pattern=[[-1, P]], channel_multiplier=1).then_inc(ident_made, 1)
            nc.gpsimd.memset(minus_half[:], -0.5).then_inc(ident_made, 1)
            chain(nc.gpsimd.memset(tri[:], 0.0))
            nc.gpsimd.affine_select(out=tri[:], in_=tri[:], compare_op=ALU.is_ge, fill=MASKED, base=0,
                                    pattern=[[-1, P]], channel_multiplier=1).then_inc(tri_made, 1)
            pool.wait_ge(ident_made, 2)
            pool.wait_ge(tri_made, 1)

            def make_mask(t):
                pool.wait_ge(mask_loaded, 16 * (t + 1))
                chain(nc.gpsimd.tensor_scalar(mask[:], mask[:].bitcast(I32), 0.0, MASKED, ALU.is_equal, ALU.mult))
                for b in range(PAIR):
                    for at in (0, KEYS - P):
                        ins = nc.gpsimd.tensor_tensor(mask[:, b, at:at + P], mask[:, b, at:at + P], tri[:],
                                                      op=ALU.add)
                ins.then_inc(mask_made, 1)

            def make_rstd(t, norm):
                pool.wait_ge(moments, ROWS * (2 * t + norm + 1))
                chain(nc.gpsimd.tensor_scalar(var_eps[:], mean_var[:, :, 1], 1.0, EPS, ALU.mult, ALU.add))
                nc.gpsimd.tensor_tensor(rstd[:], var_eps[:], minus_half[:], op=ALU.pow).then_inc(rstd_ready, 1)

            def combine_flag(seg):
                first, count = SEGMENTS[seg]
                pool.wait_ge(low_summed, first + count)
                width = count
                while width > 1:
                    width //= 2
                    a = low_sums[:, first:first + width]
                    b = low_sums[:, first + width:first + 2 * width]
                    dst = a if width > 1 else seg_sums[:, seg:seg + 1]
                    chain(nc.gpsimd.tensor_tensor(dst, a, b, op=ALU.add))
                nc.gpsimd.partition_all_reduce(seg_flags[:, seg:seg + 1], seg_sums[:, seg:seg + 1], P, RADD
                                               ).then_inc(flag_ready, 1)

            make_rstd(0, 0)
            make_mask(0)
            make_rstd(0, 1)
            combine_flag(GATE_UP)
            make_rstd(1, 0)
            combine_flag(HID1A)
            make_mask(1)
            combine_flag(HID1B)
            combine_flag(HID2A)
            combine_flag(HID2B)
            make_rstd(1, 1)
            combine_flag(DOWN)
            for t in range(2, TILES):
                make_rstd(t, 0)
                make_mask(t)
                make_rstd(t, 1)

        @block.scalar
        def _(act):
            def test_piece(n):
                act.wait_ge(loaded[n], 16)
                if n:
                    act.wait_ge(low_summed, n)
                low = weights[:, n].bitcast(U16)[:, 0:2 * PIECE:2]
                nc.scalar.activation(test_out[:], low, ACT.Copy, accum_out=low_sums[:, n:n + 1]
                                     ).then_inc(low_summed, 1)

            def evacuate_q(t):
                for c in range(EC):
                    act.wait_ge(q_turned, EC * t + c + 1)
                    nc.scalar.activation(q_cols[:, c], att[c][:], ACT.Copy, scale=SCALE).then_inc(q_evacuated, 1)

            def exponentials(t):
                act.wait_ge(neg_ready, t + 1)
                for n in range(ROWS):
                    b, cols = half(n // 2, n % 2)
                    nc.scalar.activation(probs[:, b, cols], probs[:, b, cols], ACT.Exp, bias=neg_max[:, n:n + 1],
                                         accum_out=row_sum[:, n:n + 1]).then_inc(probs_ready, 1)

            def split_xn(t):
                for c in range(EC):
                    act.wait_ge(xn_turned, EC * t + c + 1)
                    nc.scalar.activation(xn_hi[:, c], att[c][:], ACT.Copy).then_inc(xn_hi_ready, 1)

            def set_residual(t):
                act.wait_ge(x_attn_done, ROWS * (t + 1))
                if not isinstance(t, int) or t > 0:
                    act.wait_ge(out_stored, 16 * ROWS * t)
                nc.scalar.activation(residual[:], x_attn[:], ACT.Copy).then_inc(residual_set, 1)

            def hi_part(t, c):
                act.wait_ge(gated, HC * t + c + 1)
                nc.scalar.activation(h_hi[0][:, c], act32[:, c % 3], ACT.Copy).then_inc(hi_done, 1)

            def first_layer(t, tests=()):
                for c in range(HC + 1):
                    if c < HC:
                        act.wait_ge(gate_mm, HC * t + c + 1)
                        if c >= 2:
                            act.wait_ge(gated, HC * t + c - 1)
                        elif not isinstance(t, int) or t > 0:
                            act.wait_ge(result_done, ROWS * t)
                        nc.scalar.activation(gate[:, c % 2], ring[2 * c % RING][:], ACT.Silu,
                                             scale=gate_scale[:, c:c + 1]).then_inc(gate_done, 1)
                    if c >= 1:
                        hi_part(t, c - 1)
                    if c % 2 == 1 and tests:
                        test_piece(tests.pop(0))

            def gelu(t, layer, c):
                n = HC * (layer + 1) + c
                scale = (h1_scale, h2_scale)[layer]
                act.wait_ge(hid_mm, 2 * HC * t + HC * layer + c + 1)
                act.wait_ge(split, CH * t + n - 2)
                nc.scalar.activation(act32[:, n % 3], ring[(2 * HC + HC * layer + c) % RING][:], ACT.Gelu,
                                     scale=scale[:, c:c + 1]).then_inc(gelu_done, 1)

            def span(seg):
                first, count = SEGMENTS[seg]
                return first, first + count

            def tile(t, tests=None, more=True):
                tests = tests or {}
                first_layer(t, tests.get("first layer", []))
                if more:
                    evacuate_q(t + 1)
                set_residual(t)
                for c in range(HC):
                    gelu(t, 0, c)
                    if c == HC // 2 + 1 and more:
                        exponentials(t + 1)
                    for n in tests.get((0, c), []):
                        test_piece(n)
                for c in range(HC):
                    gelu(t, 1, c)
                    for n in tests.get((1, c), []):
                        test_piece(n)
                if more:
                    split_xn(t + 1)

            act.wait_ge(consts_in, 32)
            evacuate_q(0)
            exponentials(0)
            for n in range(GU_P):
                test_piece(n)
            split_xn(0)
            tests = {"first layer": list(range(*span(HID1A)))}
            for seg, layer, c in ((HID1B, 0, 0), (HID2A, 0, HC // 2), (HID2B, 1, 0), (DOWN, 1, HC // 2)):
                for n in range(*span(seg)):
                    tests.setdefault((layer, c), []).append(n)
                    c += n > span(seg)[0]
            tile(0, tests)
            with act.Fori(1, TILES - 1) as t:
                tile(t)
            tile(TILES - 1, more=False)

        @block.vector
        def _(dve):
            def norm_stats(t, norm, src, r):
                nc.vector.bn_stats(out=stats[:, r], in_=src[:, r]).then_inc(stats_step, 1)

            def wait_stats(t, norm, r):
                dve.wait_ge(stats_step, ROWS * (2 * t + norm) + r + 1)

            def norm_moments(r):
                nc.vector.bn_aggr(out=mean_var[:, r], in_=stats[:, r]).then_inc(moments, 1)

            def whole_norm(t, norm, src):
                for r in range(ROWS):
                    norm_stats(t, norm, src, r)
                for r in range(ROWS):
                    wait_stats(t, norm, r)
                    norm_moments(r)
                for r in range(ROWS):
                    normalise(t, norm, src, r)

            def normalise(t, norm, src, r):
                if r == 0:
                    dve.wait_ge(rstd_ready, 2 * t + norm + 1)
                    dve.wait_ge(moments, ROWS * (2 * t + norm + 1))
                nc.vector.tensor_scalar(xn[:, r], src[:, r], mean_var[:, r, 0:1], rstd[:, r:r + 1],
                                        ALU.subtract, ALU.mult).then_inc(xn_ready, 1)

            def wait_scores(t):
                dve.wait_ge(mask_made, t + 1)
                dve.wait_ge(scores_done, PAIR * (t + 1))

            def mask_and_max(t):
                for n in range(ROWS):
                    b, cols = half(n // 2, n % 2)
                    nc.vector.tensor_tensor_reduce(out=probs[:, b, cols], in0=att[b][:, cols], in1=mask[:, b, cols],
                                                   scale=1.0, scalar=FLOOR, op0=ALU.add, op1=ALU.max,
                                                   accum_out=row_max[:, n:n + 1]).then_inc(maxed, 1)
                dve.wait_ge(maxed, ROWS * (t + 1))
                nc.vector.tensor_scalar(neg_max[:], row_max[:], -1.0, None, ALU.mult).then_inc(neg_ready, 1)

            def evacuate_probs(t):
                for b in range(PAIR):
                    dve.wait_ge(probs_turned, PAIR * t + b + 1)
                    nc.vector.tensor_copy(probs_t[:, b], att[b][:, 0:KEYS]).then_inc(probs_evac, 1)

            def add_attention(t):
                dve.wait_ge(probs_ready, ROWS * (t + 1))
                nc.vector.reciprocal(inv_sum[:], row_sum[:]).then_inc(inv_ready, 1)
                dve.wait_ge(inv_ready, t + 1)
                if not isinstance(t, int) or t > 0:
                    dve.wait_ge(residual_set, t)
                for r in range(ROWS):
                    if r % 2 == 0:
                        dve.wait_ge(attended, PAIR * t + r // 2 + 1)
                    nc.vector.scalar_tensor_tensor(out=x_attn[:, r], in0=att[r // 2][:, (r % 2) * EMB:][:, 0:EMB],
                                                   scalar=inv_sum[:, r:r + 1], in1=x_in[:, r],
                                                   op0=ALU.mult, op1=ALU.add).then_inc(x_attn_done, 1)
                dve.wait_ge(x_attn_done, ROWS * (t + 1))

            def split_xn(t):
                for c in range(EC):
                    dve.wait_ge(xn_hi_ready, EC * t + c + 1)
                    nc.vector.tensor_tensor(xn_lo[:, c], att[c][:], xn_hi[:, c].bitcast(F32), op=ALU.subtract
                                            ).then_inc(xn_split, 1)

            def lo_part(t, n, buf, c):
                nc.vector.tensor_tensor(h_lo[buf][:, c], act32[:, n % 3], h_hi[buf][:, c].bitcast(F32),
                                        op=ALU.subtract).then_inc(split, 1)

            def first_layer(t, more):
                for c in range(HC + 1):
                    if c < HC:
                        if more and 1 <= c <= ROWS:
                            wait_stats(t + 1, 0, c - 1)
                        dve.wait_ge(up_mm, HC * t + c + 1)
                        dve.wait_ge(gate_done, HC * t + c + 1)
                        if not isinstance(t, int) or CH * t + c - 2 > 0:
                            dve.wait_ge(split, CH * t + c - 2)
                        nc.vector.scalar_tensor_tensor(out=act32[:, c % 3], in0=ring[(2 * c + 1) % RING][:],
                                                       scalar=up_scale[:, c:c + 1], in1=gate[:, c % 2],
                                                       op0=ALU.mult, op1=ALU.mult).then_inc(gated, 1)
                    if c >= 1:
                        dve.wait_ge(hi_done, HC * t + c)
                        lo_part(t, c - 1, 0, c - 1)
                    if more and c < ROWS:
                        if c == 0:
                            dve.wait_ge(x_loaded, 16 * (t + 2))
                        norm_stats(t + 1, 0, x_in, c)
                    if more and 1 <= c <= ROWS:
                        norm_moments(c - 1)
                    if more and c in (6, 7):
                        for r in (0, 1) if c == 6 else (2, 3):
                            normalise(t + 1, 0, x_in, r)

            def split_hidden(t, layer, c):
                n = HC * (layer + 1) + c
                buf = (layer + 1) % 2
                dve.wait_ge(gelu_done, 2 * HC * t + HC * layer + c + 1)
                nc.vector.tensor_copy(h_hi[buf][:, c], act32[:, n % 3]).then_inc(hi_made, 1)
                dve.wait_ge(hi_made, 2 * HC * t + HC * layer + c + 1)
                lo_part(t, n, buf, c)

            def results(t):
                dve.wait_ge(residual_set, t + 1)
                for r in range(ROWS):
                    bank = ring[(4 * HC + r) % RING]
                    dve.wait_ge(down_mm, ROWS * t + r + 1)
                    if r >= 2:
                        dve.wait_ge(result_done, ROWS * t + r - 1)
                    nc.vector.tensor_tensor(gate[:, r % 2, 0:EMB], bank[:, 0:EMB], down_scale[:], op=ALU.mult
                                            ).then_inc(down_free, 1)
                    dve.wait_ge(down_free, ROWS * (t + 1) + r + 1)
                    nc.vector.tensor_tensor(residual[:, r], residual[:, r], gate[:, r % 2, 0:EMB], op=ALU.add
                                            ).then_inc(result_done, 1)

            def tile(t, more=True):
                first_layer(t, more)
                middle = HC // 2
                for c in range(HC):
                    if more and c == middle:
                        wait_scores(t + 1)
                    split_hidden(t, 0, c)
                    if more and c == middle:
                        mask_and_max(t + 1)
                if more:
                    evacuate_probs(t + 1)
                for c in range(HC):
                    if more and c == middle:
                        wait_stats(t + 1, 1, ROWS - 1)
                    split_hidden(t, 1, c)
                    if more and c == middle - 1:
                        add_attention(t + 1)
                        for r in range(ROWS):
                            norm_stats(t + 1, 1, x_attn, r)
                    if more and c == middle:
                        for r in range(ROWS):
                            norm_moments(r)
                    if more and c == middle + 1:
                        for r in range(ROWS):
                            normalise(t + 1, 1, x_attn, r)
                if more:
                    split_xn(t + 1)
                results(t)

            nc.vector.memset(gate[:, 0, 0:8], 0.0).then_inc(down_free, ROWS)
            dve.wait_ge(consts_in, 32)
            dve.wait_ge(x_loaded, 16)
            whole_norm(0, 0, x_in)
            wait_scores(0)
            mask_and_max(0)
            evacuate_probs(0)
            add_attention(0)
            whole_norm(0, 1, x_attn)
            split_xn(0)
            tile(0)
            with dve.Fori(1, TILES - 1) as t:
                tile(t)
            tile(TILES - 1, more=False)

        @block.tensor
        def _(pe):
            def turn_rows(t, norm, done):
                for c in range(EC):
                    for r in range(ROWS):
                        if c == 0:
                            pe.wait_ge(xn_ready, ROWS * (2 * t + norm) + r + 1)
                        ins = nc.tensor.transpose(att[c][:, r * P:(r + 1) * P], xn[:, r, c * P:(c + 1) * P],
                                                  ident[:])
                    ins.then_inc(done, 1)

            def scores(t):
                pe.wait_ge(q_evacuated, EC * (t + 1))
                pe.wait_ge(ctx_loaded, 32 * (t + 1))
                for b in range(PAIR):
                    for q in range(2):
                        _, cols = half(b, q)
                        for c in range(EC):
                            ins = nc.tensor.matmul(att[b][:, cols],
                                                   q_cols[:, c, b * SEQ + q * P:b * SEQ + (q + 1) * P],
                                                   ctx_cols[:, c, b * SEQ:b * SEQ + (q + 1) * P],
                                                   start=(c == 0), stop=(c == EC - 1))
                    ins.then_inc(scores_done, 1)

            def turn_probs(t):
                for b in range(PAIR):
                    pe.wait_ge(probs_ready, ROWS * t + 2 * b + 2)
                    for n in range(KEYS // P):
                        ins = nc.tensor.transpose(att[b][:, n * P:(n + 1) * P], probs[:, b, n * P:(n + 1) * P],
                                                  ident[:])
                    ins.then_inc(probs_turned, 1)

            def attend(t):
                pe.wait_ge(probs_evac, PAIR * (t + 1))
                for b in range(PAIR):
                    for q in range(2):
                        for k in range(q + 1):
                            n = k + q
                            ins = nc.tensor.matmul(att[b][:, q * EMB:(q + 1) * EMB],
                                                   probs_t[:, b, n * P:(n + 1) * P], ctx_rows[:, 2 * b + k],
                                                   start=(k == 0), stop=(k == q))
                    ins.then_inc(attended, 1)

            def gate_and_up(t, dt):
                for c in range(HC):
                    if c == 0:
                        pe.wait_ge(xn_split, EC * (t + 1))
                    elif c in (1, 2):
                        pe.wait_ge(down_free, ROWS * t + 2 * c)
                    else:
                        pe.wait_ge(gated, HC * t + c - 2)
                    for which, done in ((0, gate_mm), (1, up_mm)):
                        bank = ring[(2 * c + which) % RING]
                        for k in range(EC):
                            at = ((c % 2 * 2 + which) * EC + k) * P
                            w = weights[:, c // 2, at:at + P].bitcast(dt)
                            for part in (xn_hi, xn_lo):
                                ins = nc.tensor.matmul(bank[:], w, part[:, k].bitcast(dt),
                                                       start=(k == 0 and part is xn_hi),
                                                       stop=(k == EC - 1 and part is xn_lo))
                        ins.then_inc(done, 1)

            def hidden(t, layer, chunks, dt):
                src = layer % 2
                for c in chunks:
                    if c == 0 and layer == 0:
                        pe.wait_ge(gated, HC * t + HC - 2)
                    elif c == 0:
                        pe.wait_ge(gelu_done, 2 * HC * t + HC - RING + 1)
                    elif c >= RING:
                        pe.wait_ge(gelu_done, 2 * HC * t + HC * layer + c - RING + 1)
                    bank = ring[(2 * HC + HC * layer + c) % RING]
                    for k in range(HC):
                        if c == 0:
                            pe.wait_ge(split, CH * t + HC * layer + k + 1)
                        w = weights[:, GU_P + H_P * layer + c, k * P:(k + 1) * P].bitcast(dt)
                        for part in (h_hi[src], h_lo[src]):
                            ins = nc.tensor.matmul(bank[:], w, part[:, k].bitcast(dt),
                                                   start=(k == 0 and part is h_hi[src]),
                                                   stop=(k == HC - 1 and part is h_lo[src]))
                    ins.then_inc(hid_mm, 1)

            def down(t, dt):
                for r in range(ROWS):
                    bank = ring[(4 * HC + r) % RING]
                    if r == 0:
                        pe.wait_ge(gelu_done, 2 * HC * t + 2 * HC - RING + 1)
                    for k in range(HC):
                        if r == 0:
                            pe.wait_ge(split, CH * t + 2 * HC + k + 1)
                        n, at = divmod(k * EMB, PIECE)
                        w = weights[:, GU_P + 2 * H_P + n, at:at + EMB].bitcast(dt)
                        for part in (h_hi[0], h_lo[0]):
                            ins = nc.tensor.matmul(bank[:, 0:EMB], part[:, k, r * P:(r + 1) * P].bitcast(dt), w,
                                                   start=(k == 0 and part is h_hi[0]),
                                                   stop=(k == HC - 1 and part is h_lo[0]))
                    ins.then_inc(down_mm, 1)

            def segment(seg, products):
                pe.wait_ge(flag_ready, seg + 1)
                flag = pe.value_load(seg_flags[0:1, seg:seg + 1].bitcast(I32), min_val=0, max_val=2**31 - 1)
                with pe.If(flag == 0):
                    products(F32R)
                with pe.Else():
                    products(F32)

            def tile(t, more=True):
                halves = range(HC // 2), range(HC // 2, HC)
                segment(GATE_UP, lambda dt: gate_and_up(t, dt))
                if more:
                    turn_rows(t + 1, 0, q_turned)
                segment(HID1A, lambda dt: hidden(t, 0, halves[0], dt))
                if more:
                    scores(t + 1)
                segment(HID1B, lambda dt: hidden(t, 0, halves[1], dt))
                if more:
                    turn_probs(t + 1)
                segment(HID2A, lambda dt: hidden(t, 1, halves[0], dt))
                if more:
                    attend(t + 1)
                segment(HID2B, lambda dt: hidden(t, 1, halves[1], dt))
                if more:
                    turn_rows(t + 1, 1, xn_turned)
                segment(DOWN, lambda dt: down(t, dt))

            pe.wait_ge(ident_made, 2)
            turn_rows(0, 0, q_turned)
            scores(0)
            turn_probs(0)
            attend(0)
            turn_rows(0, 1, xn_turned)
            with pe.Fori(0, TILES - 1) as t:
                tile(t)
            tile(TILES - 1, more=False)


def kernel(**inputs):
    import numpy as np
    import concourse.bacc as bacc
    from concourse.bass_utils import run_bass_kernel_spmd

    def chunked(w, chunks):
        w = np.asarray(w)
        return w.reshape(chunks, -1, w.shape[1] // P, P).transpose(0, 3, 2, 1)

    x = np.asarray(inputs["x"]).reshape(BATCH * SEQ, EMB)
    ctx = np.asarray(inputs["ctx_1024"])
    key_mask = np.asarray(inputs["mask_BxS2_ik1"])
    gate_up = np.stack([chunked(inputs["L0_ffn_w1_w"], HC), chunked(inputs["L0_ffn_w2_w"], HC)], axis=2)
    gate_up = gate_up.reshape(GU_P, 2, P, PIECE // 2).transpose(0, 2, 1, 3).reshape(GU_P, P, PIECE)
    hidden = [chunked(inputs[f"L0_ffn_h{n}_w"], HC).reshape(H_P, P, PIECE) for n in (1, 2)]
    down = chunked(inputs["L0_ffn_w3_w"], 1).reshape(P, DOWN_P, PIECE).transpose(1, 0, 2)
    scales = np.stack([np.asarray(inputs[f"L0_ffn_{n}_s"]).reshape(HC, P).T for n in ("w1", "w2", "h1", "h2")], axis=1)
    arrays = {
        "in_x": x,
        "in_ctx_rows": ctx.reshape(BATCH * SEQ, EMB),
        "in_ctx_cols": ctx.reshape(TILES, TOK, EC, P).transpose(0, 3, 2, 1),
        "in_mask": np.concatenate([key_mask[:, 0:P], key_mask], axis=1).reshape(TILES, PAIR * KEYS),
        "in_weights": np.concatenate([gate_up, *hidden, down]),
        "in_scales": scales,
        "in_down_scale": np.asarray(inputs["L0_ffn_w3_s"]),
    }
    arrays = {k: np.ascontiguousarray(a) for k, a in arrays.items()}
    nc = bacc.Bacc("TRN2", target_bir_lowering=False, num_devices=1)
    args = [nc.dram_tensor(k, a.shape, mybir.dt.from_np(a.dtype), kind="ExternalInput").ap() for k, a in arrays.items()]
    out = nc.dram_tensor("out_dram", (BATCH * SEQ, EMB), F32, kind="ExternalOutput").ap()
    xattn_ffn(nc, *args, out)
    results = run_bass_kernel_spmd(nc, [arrays], core_ids=[0])
    return results.results[0]["out_dram"].reshape(BATCH, SEQ, EMB)
```

```python
from contextlib import ExitStack

import concourse.bass as bass
from concourse import mybir

F32 = mybir.dt.float32
F32R = mybir.dt.float32r
BF16 = mybir.dt.bfloat16
I32 = mybir.dt.int32
U16 = mybir.dt.uint16
ALU = mybir.AluOpType
ACT = mybir.ActivationFunctionType
RADD = bass.bass_isa.ReduceOp.add

P = 128
BATCH, SEQ, EMB, HID = 8, 256, 256, 1024
PAIR = 2
TOK = PAIR * SEQ
TILES = BATCH // PAIR
ROWS = TOK // P
EC = EMB // P
HC = HID // P
KEYS = P + SEQ
EPS = 1e-5
SCALE = float(EMB) ** -0.5
MASKED = -1.5e38
FLOOR = -1.0e37

PIECE = 1024
GU_P = 2 * EC * HID // PIECE
H_P = HC * HID // PIECE
DOWN_P = HC * EMB // PIECE
PIECES = GU_P + 2 * H_P + DOWN_P
GATE_UP_A, GATE_UP_B, HID1A, HID1B, HID2A, HID2B, HID2C, DOWN = range(8)
HID1_CHUNKS = {HID1A: (0, 4), HID1B: (4, 8)}
HID2_CHUNKS = {HID2A: (0, 3), HID2B: (3, 5), HID2C: (5, 8)}
SPANS = {GATE_UP_A: (0, GU_P // 2), GATE_UP_B: (GU_P // 2, GU_P), DOWN: (PIECES - DOWN_P, PIECES)}
SPANS.update({seg: (GU_P + a, GU_P + b) for seg, (a, b) in HID1_CHUNKS.items()})
SPANS.update({seg: (GU_P + H_P + a, GU_P + H_P + b) for seg, (a, b) in HID2_CHUNKS.items()})
RING = 6
CH = 3 * HC


def xattn_ffn(nc, x, ctx_rows_d, ctx_cols_d, mask_d, weights_d, scales_d, down_scale_d, out):
    staged_d = nc.dram_tensor("weights_staged", [PIECES, P, PIECE], F32).ap()
    x_v = x.rearrange("(t r p) d -> t p r d", p=P, r=ROWS)
    ctx_v = ctx_rows_d.rearrange("(t r p) d -> t p r d", p=P, r=ROWS)
    out_v = out.rearrange("(t r p) d -> t p r d", p=P, r=ROWS)

    stack = ExitStack()
    with stack:
        def sb(name, shape, dt=F32):
            return stack.enter_context(nc.sbuf_tensor(name, shape, dt))

        def sem(name):
            return stack.enter_context(nc.semaphore(name))

        weights = sb("weights", [P, PIECES, PIECE], F32R)
        h_hi = [sb(f"h_hi{n}", [P, HC, TOK], F32R) for n in range(2)]
        h_lo = [sb(f"h_lo{n}", [P, HC, TOK], F32R) for n in range(2)]
        xn_hi = sb("xn_hi", [P, EC, TOK], F32R)
        xn_lo = sb("xn_lo", [P, EC, TOK], F32R)
        x_in = sb("x_in", [P, ROWS, EMB])
        x_attn = sb("x_attn", [P, ROWS, EMB])
        residual = sb("residual", [P, ROWS, EMB])
        ctx_rows = sb("ctx_rows", [P, ROWS, EMB])
        ctx_cols = sb("ctx_cols", [P, EC, TOK])
        mask = sb("mask", [P, PAIR, KEYS])
        work = sb("work", [P, ROWS * EMB])
        turned = sb("turned", [P, EC * TOK])
        gate = sb("gate", [P, 2, TOK])
        act32 = sb("act32", [P, 3, TOK])
        down_scale = sb("down_scale", [P, EMB])
        scales = sb("scales", [P, 4, HC])
        ident = sb("ident", [P, P])
        tri = sb("tri", [P, P])
        scaled = sb("scaled", [P, 2, EMB])
        low_sums = sb("low_sums", [P, PIECES])
        seg_flags = sb("seg_flags", [P, len(SPANS)])
        stats = sb("stats", [P, ROWS, 6])
        mean_var = sb("mean_var", [P, ROWS, 2])
        var_eps = sb("var_eps", [P, ROWS])
        rstd = sb("rstd", [P, ROWS])
        minus_half = sb("minus_half", [P, ROWS])
        row_max = sb("row_max", [P, ROWS])
        neg_max = sb("neg_max", [P, ROWS])
        row_sum = sb("row_sum", [P, ROWS])
        warm_in = sb("warm_in", [P, 1])
        warm = sb("warm", [P, 2])
        inv_sum = sb("inv_sum", [P, ROWS])

        xn = work[:].rearrange("p (r d) -> p r d", r=ROWS)
        probs = work[:, 0:PAIR * KEYS].rearrange("p (b k) -> p b k", b=PAIR)
        q_cols = turned[:].rearrange("p (b c t) -> p b c t", b=PAIR, c=EC)
        test_out = scaled[:].rearrange("p n d -> p (n d)").bitcast(BF16)
        probs_t = turned[:, 0:PAIR * KEYS].rearrange("p (b k) -> p b k", b=PAIR)
        gate_scale, up_scale, h1_scale, h2_scale = (scales[:, n] for n in range(4))

        att = [stack.enter_context(nc.psum_tensor(f"att{n}", [P, 512], F32)) for n in range(2)]
        ring = [stack.enter_context(nc.psum_tensor(f"ring{n}", [P, 512], F32)) for n in range(RING)]

        staged = [sem(f"staged{n}") for n in range(PIECES)]
        loaded = [sem(f"loaded{n}") for n in range(PIECES)]
        consts_in = sem("consts_in")
        x_loaded = sem("x_loaded")
        ctx_loaded = sem("ctx_loaded")
        mask_loaded = sem("mask_loaded")
        out_stored = sem("out_stored")
        ident_made = sem("ident_made")
        tri_made = sem("tri_made")
        pool_step = sem("pool_step")
        rstd_ready = sem("rstd_ready")
        flag_ready = sem("flag_ready")
        low_summed = sem("low_summed")
        q_evacuated = sem("q_evacuated")
        probs_ready = sem("probs_ready")
        xn_hi_ready = sem("xn_hi_ready")
        residual_set = sem("residual_set")
        gate_done = sem("gate_done")
        hi_done = sem("hi_done")
        gelu_done = sem("gelu_done")
        stats_step = sem("stats_step")
        moments = sem("moments")
        xn_ready = sem("xn_ready")
        maxed = sem("maxed")
        mask_step = sem("mask_step")
        mask_made = sem("mask_made")
        neg_ready = sem("neg_ready")
        inv_ready = sem("inv_ready")
        probs_evac = sem("probs_evac")
        x_attn_done = sem("x_attn_done")
        xn_split = sem("xn_split")
        gated = sem("gated")
        hi_made = sem("hi_made")
        split = sem("split")
        down_free = sem("down_free")
        result_done = sem("result_done")
        q_turned = sem("q_turned")
        scores_done = sem("scores_done")
        probs_turned = sem("probs_turned")
        attended = sem("attended")
        xn_turned = sem("xn_turned")
        gate_mm = sem("gate_mm")
        up_mm = sem("up_mm")
        hid_mm = sem("hid_mm")
        down_mm = sem("down_mm")

        def half(b, q):
            return (b, slice(0, P)) if q == 0 else (b, slice(P, KEYS))

        block = stack.enter_context(nc.Block())

        @block.sync
        def _(sp):
            def load_context(t):
                sp.dma_start(ctx_cols[:], ctx_cols_d[t]).then_inc(ctx_loaded, 16)
                sp.dma_start(ctx_rows[:], ctx_v[t]).then_inc(ctx_loaded, 16)

            def load_mask(t):
                sp.dma_start(mask[:].bitcast(I32), mask_d[t].partition_broadcast(P)).then_inc(mask_loaded, 16)

            def load_next(t):
                sp.wait_ge(x_attn_done, ROWS * t)
                sp.dma_start(x_in[:], x_v[t]).then_inc(x_loaded, 16)
                load_context(t)
                sp.wait_ge(maxed, ROWS * t)
                load_mask(t)

            def stage(n):
                sp.dma_start(staged_d[n], weights_d[n]).then_inc(staged[n], 16)

            def load_piece(n):
                sp.wait_ge(staged[n], 16)
                sp.dma_start(weights[:, n].bitcast(F32), staged_d[n]).then_inc(loaded[n], 16)

            def store(t):
                for r in range(ROWS):
                    sp.wait_ge(result_done, ROWS * t + r + 1)
                    sp.dma_start(out_v[t][:, r], residual[:, r]).then_inc(out_stored, 16)

            ahead = 4
            sp.dma_start(x_in[:], x_v[0]).then_inc(x_loaded, 16)
            load_mask(0)
            sp.dma_start(ctx_cols[:], ctx_cols_d[0]).then_inc(ctx_loaded, 16)
            stage(0)
            stage(1)
            sp.dma_start(ctx_rows[:], ctx_v[0]).then_inc(ctx_loaded, 16)
            sp.dma_start(scales[:], scales_d).then_inc(consts_in, 16)
            sp.dma_start(down_scale[:], down_scale_d.partition_broadcast(P)).then_inc(consts_in, 16)
            stage(2)
            stage(3)
            for n in range(PIECES):
                load_piece(n)
                if n + ahead < PIECES:
                    stage(n + ahead)
                if n == SPANS[HID1A][1] - 1:
                    load_next(1)
            with sp.Fori(0, TILES - 2) as t:
                load_next(t + 2)
                store(t)
            for t in range(TILES - 2, TILES):
                store(t)
            sp.wait_ge(out_stored, 16 * ROWS * TILES)

        @block.gpsimd
        def _(pool):
            steps = [0]

            def chain(ins):
                ins.then_inc(pool_step, 1)
                steps[0] += 1
                pool.wait_ge(pool_step, steps[0])

            chain(nc.gpsimd.memset(ident[:], 0.0))
            nc.gpsimd.affine_select(out=ident[:], in_=ident[:], compare_op=ALU.not_equal, fill=1.0, base=0,
                                    pattern=[[-1, P]], channel_multiplier=1).then_inc(ident_made, 1)
            nc.gpsimd.memset(minus_half[:], -0.5).then_inc(ident_made, 1)
            chain(nc.gpsimd.memset(tri[:], 0.0))
            nc.gpsimd.affine_select(out=tri[:], in_=tri[:], compare_op=ALU.is_ge, fill=MASKED, base=0,
                                    pattern=[[-1, P]], channel_multiplier=1).then_inc(tri_made, 1)
            pool.wait_ge(ident_made, 2)

            def make_rstd(t, norm, rows=range(ROWS)):
                pool.wait_ge(moments, ROWS * (2 * t + norm) + rows[-1] + 1)
                cols = slice(rows[0], rows[-1] + 1)
                chain(nc.gpsimd.tensor_scalar(var_eps[:, cols], mean_var[:, cols, 1], 1.0, EPS, ALU.mult, ALU.add))
                nc.gpsimd.tensor_tensor(rstd[:, cols], var_eps[:, cols], minus_half[:, cols], op=ALU.pow
                                        ).then_inc(rstd_ready, len(rows))

            def combine_flag(seg):
                first, end = SPANS[seg]
                pool.wait_ge(low_summed, end)
                while end - first > 1:
                    h = (end - first) // 2
                    chain(nc.gpsimd.tensor_tensor(low_sums[:, first:first + h], low_sums[:, first:first + h],
                                                  low_sums[:, end - h:end], op=ALU.add))
                    end -= h
                nc.gpsimd.partition_all_reduce(seg_flags[:, seg:seg + 1], low_sums[:, first:first + 1], P, RADD
                                               ).then_inc(flag_ready, 1)

            for norm in range(2):
                for b in range(PAIR):
                    make_rstd(0, norm, range(2 * b, 2 * b + 2))
                if norm == 0:
                    combine_flag(GATE_UP_A)
            combine_flag(GATE_UP_B)
            combine_flag(HID1A)
            make_rstd(1, 0)
            for seg in (HID1B, HID2A, HID2B, HID2C):
                combine_flag(seg)
            make_rstd(1, 1)
            combine_flag(DOWN)
            for t in range(2, TILES):
                make_rstd(t, 0)
                make_rstd(t, 1)

        @block.scalar
        def _(act):
            def test_piece(n):
                act.wait_ge(loaded[n], 16)
                if n:
                    act.wait_ge(low_summed, n)
                low = weights[:, n].bitcast(U16)[:, 0:2 * PIECE:2]
                nc.scalar.activation(test_out, low, ACT.Copy, accum_out=low_sums[:, n:n + 1]
                                     ).then_inc(low_summed, 1)

            def evacuate_q(t):
                for b in range(PAIR):
                    act.wait_ge(q_turned, PAIR * t + b + 1)
                    nc.scalar.activation(turned[:, b * 512:(b + 1) * 512], att[b][:], ACT.Copy, scale=SCALE
                                         ).then_inc(q_evacuated, 1)

            def exponentials(t):
                for n in range(ROWS):
                    b, cols = half(n // 2, n % 2)
                    if n % 2 == 0:
                        act.wait_ge(neg_ready, PAIR * t + b + 1)
                    nc.scalar.activation(probs[:, b, cols], probs[:, b, cols], ACT.Exp, bias=neg_max[:, n:n + 1],
                                         accum_out=row_sum[:, n:n + 1]).then_inc(probs_ready, 1)

            def split_xn(t):
                for b in range(PAIR):
                    act.wait_ge(xn_turned, PAIR * t + b + 1)
                    nc.scalar.activation(xn_hi[:, :, b * SEQ:(b + 1) * SEQ],
                                         att[b][:].rearrange("p (c t) -> p c t", c=EC), ACT.Copy
                                         ).then_inc(xn_hi_ready, 1)

            def set_residual(t):
                act.wait_ge(x_attn_done, ROWS * (t + 1))
                if not isinstance(t, int) or t > 0:
                    act.wait_ge(out_stored, 16 * ROWS * t)
                nc.scalar.activation(residual[:], x_attn[:], ACT.Copy).then_inc(residual_set, 1)

            def hi_part(t, c):
                act.wait_ge(gated, HC * t + c + 1)
                nc.scalar.activation(h_hi[0][:, c], act32[:, c % 3], ACT.Copy).then_inc(hi_done, 1)

            def first_layer(t, tests=()):
                for c in range(HC + 1):
                    if c < HC:
                        act.wait_ge(gate_mm, HC * t + c + 1)
                        if c >= 2 or not isinstance(t, int) or t > 0:
                            act.wait_ge(gated, HC * t + c - 1)
                        nc.scalar.activation(gate[:, c % 2], ring[2 * c % RING][:], ACT.Silu,
                                             scale=gate_scale[:, c:c + 1]).then_inc(gate_done, 1)
                    if c >= 1:
                        hi_part(t, c - 1)
                    if c % 2 == 0 and tests:
                        test_piece(tests.pop(0))

            def gelu(t, layer, c):
                n = HC * (layer + 1) + c
                scale = (h1_scale, h2_scale)[layer]
                act.wait_ge(hid_mm, 2 * HC * t + HC * layer + c + 1)
                act.wait_ge(split, CH * t + n - 2)
                nc.scalar.activation(act32[:, n % 3], ring[(2 * HC + HC * layer + c) % RING][:], ACT.Gelu,
                                     scale=scale[:, c:c + 1]).then_inc(gelu_done, 1)

            def tile(t, tests=None, more=True):
                tests = tests or {}
                first_layer(t, tests.get("first layer", []))
                for layer in range(2):
                    for c in range(HC):
                        gelu(t, layer, c)
                        if (layer, c) == (0, 0):
                            set_residual(t)
                        for n in tests.get((layer, c), []):
                            test_piece(n)
                        if more and (layer, c) == (0, HID1_CHUNKS[HID1A][1] - 1):
                            evacuate_q(t + 1)
                        if more and (layer, c) == (0, HC - 1):
                            exponentials(t + 1)
                if more:
                    split_xn(t + 1)
                    nc.scalar.activation(warm[:, 1:2], warm_in[:], ACT.Silu)

            act.wait_ge(down_free, ROWS)
            nc.scalar.activation(warm[:, 0:1], warm_in[:], ACT.Exp)
            evacuate_q(0)
            exponentials(0)
            for n in range(*SPANS[GATE_UP_A]):
                test_piece(n)
            split_xn(0)
            for n in range(*SPANS[GATE_UP_B]):
                test_piece(n)
            act.wait_ge(consts_in, 32)
            tests = {"first layer": list(range(*SPANS[HID1A]))}
            n = SPANS[HID1A][1]
            for at in ((0, 0), (0, 1), (0, 2), (0, 2), (0, 4), (0, 5), (0, 6), (1, 0), (1, 1), (1, 2), (1, 3), (1, 3),
                       (1, 5), (1, 6)):
                tests.setdefault(at, []).append(n)
                n += 1
            tile(0, tests)
            with act.Fori(1, TILES - 1) as t:
                tile(t)
            tile(TILES - 1, more=False)

        @block.vector
        def _(dve):
            def norm_stats(r, src):
                nc.vector.bn_stats(out=stats[:, r], in_=src[:, r]).then_inc(stats_step, 1)

            def wait_stats(t, norm, r):
                dve.wait_ge(stats_step, ROWS * (2 * t + norm) + r + 1)

            def norm_moments(r):
                nc.vector.bn_aggr(out=mean_var[:, r], in_=stats[:, r]).then_inc(moments, 1)

            def normalise(t, norm, src, r):
                if r % 2 == 0:
                    dve.wait_ge(moments, ROWS * (2 * t + norm) + r + 2)
                    dve.wait_ge(rstd_ready, ROWS * (2 * t + norm) + (r + 2 if isinstance(t, int) and t == 0 else ROWS))
                nc.vector.tensor_scalar(xn[:, r], src[:, r], mean_var[:, r, 0:1], rstd[:, r:r + 1],
                                        ALU.subtract, ALU.mult).then_inc(xn_ready, 1)

            def make_mask(t):
                dve.wait_ge(mask_loaded, 16 * (t + 1))
                nc.vector.tensor_scalar(mask[:], mask[:].bitcast(I32), 0.0, MASKED, ALU.is_equal, ALU.mult
                                        ).then_inc(mask_step, 1)
                dve.wait_ge(mask_step, t + 1)
                for b in range(PAIR):
                    for at in (0, KEYS - P):
                        ins = nc.vector.tensor_tensor(mask[:, b, at:at + P], mask[:, b, at:at + P], tri[:],
                                                      op=ALU.add)
                ins.then_inc(mask_made, 1)

            def wait_scores(t):
                dve.wait_ge(mask_made, t + 1)
                dve.wait_ge(scores_done, PAIR * (t + 1))

            def mask_and_max(t, b):
                for n in (2 * b, 2 * b + 1):
                    _, cols = half(b, n % 2)
                    nc.vector.tensor_tensor_reduce(out=probs[:, b, cols], in0=att[b][:, cols], in1=mask[:, b, cols],
                                                   scale=1.0, scalar=FLOOR, op0=ALU.add, op1=ALU.max,
                                                   accum_out=row_max[:, n:n + 1]).then_inc(maxed, 1)
                dve.wait_ge(maxed, ROWS * t + 2 * b + 2)
                nc.vector.tensor_scalar(neg_max[:, 2 * b:2 * b + 2], row_max[:, 2 * b:2 * b + 2], -1.0, None, ALU.mult
                                        ).then_inc(neg_ready, 1)

            def evacuate_probs(t):
                for b in range(PAIR):
                    dve.wait_ge(probs_turned, PAIR * t + b + 1)
                    nc.vector.tensor_copy(probs_t[:, b], att[b][:, 0:KEYS]).then_inc(probs_evac, 1)

            def add_attention(t, b):
                dve.wait_ge(probs_ready, ROWS * t + 2 * b + 2)
                nc.vector.reciprocal(inv_sum[:, 2 * b:2 * b + 2], row_sum[:, 2 * b:2 * b + 2]).then_inc(inv_ready, 1)
                dve.wait_ge(inv_ready, PAIR * t + b + 1)
                if b == 0 and (not isinstance(t, int) or t > 0):
                    dve.wait_ge(residual_set, t)
                dve.wait_ge(attended, PAIR * t + b + 1)
                for r in (2 * b, 2 * b + 1):
                    nc.vector.scalar_tensor_tensor(out=x_attn[:, r], in0=att[b][:, (r % 2) * EMB:][:, 0:EMB],
                                                   scalar=inv_sum[:, r:r + 1], in1=x_in[:, r],
                                                   op0=ALU.mult, op1=ALU.add).then_inc(x_attn_done, 1)
                dve.wait_ge(x_attn_done, ROWS * t + 2 * b + 2)
                for r in (2 * b, 2 * b + 1):
                    norm_stats(r, x_attn)

            def split_xn(t):
                for b in range(PAIR):
                    toks = slice(b * SEQ, (b + 1) * SEQ)
                    dve.wait_ge(xn_hi_ready, PAIR * t + b + 1)
                    nc.vector.tensor_tensor(xn_lo[:, :, toks], att[b][:].rearrange("p (c t) -> p c t", c=EC),
                                            xn_hi[:, :, toks].bitcast(F32), op=ALU.subtract).then_inc(xn_split, 1)

            def lo_part(t, n, buf, c):
                nc.vector.tensor_tensor(h_lo[buf][:, c], act32[:, n % 3], h_hi[buf][:, c].bitcast(F32),
                                        op=ALU.subtract).then_inc(split, 1)

            def first_layer(t):
                for c in range(HC + 1):
                    if c < HC:
                        dve.wait_ge(up_mm, HC * t + c + 1)
                        dve.wait_ge(gate_done, HC * t + c + 1)
                        if not isinstance(t, int) or CH * t + c - 2 > 0:
                            dve.wait_ge(split, CH * t + c - 2)
                        nc.vector.scalar_tensor_tensor(out=act32[:, c % 3], in0=ring[(2 * c + 1) % RING][:],
                                                       scalar=up_scale[:, c:c + 1], in1=gate[:, c % 2],
                                                       op0=ALU.mult, op1=ALU.mult).then_inc(gated, 1)
                    if c >= 1:
                        dve.wait_ge(hi_done, HC * t + c)
                        lo_part(t, c - 1, 0, c - 1)

            def split_hidden(t, layer, c):
                n = HC * (layer + 1) + c
                buf = (layer + 1) % 2
                dve.wait_ge(gelu_done, 2 * HC * t + HC * layer + c + 1)
                nc.vector.tensor_copy(h_hi[buf][:, c], act32[:, n % 3]).then_inc(hi_made, 1)
                dve.wait_ge(hi_made, 2 * HC * t + HC * layer + c + 1)
                lo_part(t, n, buf, c)

            def results(t):
                dve.wait_ge(residual_set, t + 1)
                for r in range(ROWS):
                    bank = ring[(4 * HC + r) % RING]
                    dve.wait_ge(down_mm, ROWS * t + r + 1)
                    if r >= 2:
                        dve.wait_ge(result_done, ROWS * t + r - 1)
                    nc.vector.tensor_tensor(scaled[:, r % 2], bank[:, 0:EMB], down_scale[:], op=ALU.mult
                                            ).then_inc(down_free, 1)
                    dve.wait_ge(down_free, ROWS * (t + 1) + r + 1)
                    nc.vector.tensor_tensor(residual[:, r], residual[:, r], scaled[:, r % 2], op=ALU.add
                                            ).then_inc(result_done, 1)

            def tile(t, more=True):
                first_layer(t)
                for layer in range(2):
                    for c in range(HC):
                        at = (layer, c) if more else None
                        if at == (0, 1):
                            wait_stats(t + 1, 0, ROWS - 1)
                        if at == (0, HC - 1):
                            wait_scores(t + 1)
                        if at == (1, HID2_CHUNKS[HID2C][0]):
                            wait_stats(t + 1, 1, ROWS - 1)
                        split_hidden(t, layer, c)
                        if at == (0, 0):
                            dve.wait_ge(x_loaded, 16 * (t + 2))
                            for r in range(ROWS):
                                norm_stats(r, x_in)
                        if at in ((0, 1), (1, HID2_CHUNKS[HID2C][0])):
                            for r in range(ROWS):
                                norm_moments(r)
                        if at == (0, 1):
                            make_mask(t + 1)
                        if at == (0, 2):
                            for r in range(ROWS):
                                normalise(t + 1, 0, x_in, r)
                        if at == (0, HC - 1):
                            for b in range(PAIR):
                                mask_and_max(t + 1, b)
                        if at == (1, HID2_CHUNKS[HID2A][1] - 1):
                            evacuate_probs(t + 1)
                        if at == (1, HID2_CHUNKS[HID2B][1] - 1):
                            for b in range(PAIR):
                                add_attention(t + 1, b)
                        if at == (1, HID2_CHUNKS[HID2C][0] + 1):
                            for r in range(ROWS):
                                normalise(t + 1, 1, x_attn, r)
                if more:
                    split_xn(t + 1)
                results(t)

            nc.vector.memset(warm_in[:], 0.0).then_inc(down_free, ROWS)
            dve.wait_ge(x_loaded, 16)
            for b in range(PAIR):
                for r in (2 * b, 2 * b + 1):
                    norm_stats(r, x_in)
                for r in (2 * b, 2 * b + 1):
                    wait_stats(0, 0, r)
                    norm_moments(r)
            for r in range(2):
                normalise(0, 0, x_in, r)
            dve.wait_ge(tri_made, 1)
            make_mask(0)
            for r in range(2, ROWS):
                normalise(0, 0, x_in, r)
            dve.wait_ge(mask_made, 1)
            for b in range(PAIR):
                dve.wait_ge(scores_done, b + 1)
                mask_and_max(0, b)
            evacuate_probs(0)
            for b in range(PAIR):
                add_attention(0, b)
                for r in (2 * b, 2 * b + 1):
                    wait_stats(0, 1, r)
                    norm_moments(r)
            for r in range(ROWS):
                normalise(0, 1, x_attn, r)
            split_xn(0)
            dve.wait_ge(consts_in, 32)
            tile(0)
            with dve.Fori(1, TILES - 1) as t:
                tile(t)
            tile(TILES - 1, more=False)

        @block.tensor
        def _(pe):
            def turn_rows(t, norm, done):
                for b in range(PAIR):
                    for r in (2 * b, 2 * b + 1):
                        pe.wait_ge(xn_ready, ROWS * (2 * t + norm) + r + 1)
                        for c in range(EC):
                            at = c * SEQ + r % 2 * P
                            ins = nc.tensor.transpose(att[b][:, at:at + P], xn[:, r, c * P:(c + 1) * P], ident[:])
                    ins.then_inc(done, 1)

            def scores(t):
                pe.wait_ge(ctx_loaded, 32 * (t + 1))
                for b in range(PAIR):
                    pe.wait_ge(q_evacuated, PAIR * t + b + 1)
                    for q in range(2):
                        _, cols = half(b, q)
                        for c in range(EC):
                            ins = nc.tensor.matmul(att[b][:, cols], q_cols[:, b, c, q * P:(q + 1) * P],
                                                   ctx_cols[:, c, b * SEQ:b * SEQ + (q + 1) * P],
                                                   start=(c == 0), stop=(c == EC - 1))
                    ins.then_inc(scores_done, 1)

            def turn_probs(t):
                for b in range(PAIR):
                    pe.wait_ge(probs_ready, ROWS * t + 2 * b + 2)
                    for n in range(KEYS // P):
                        ins = nc.tensor.transpose(att[b][:, n * P:(n + 1) * P], probs[:, b, n * P:(n + 1) * P],
                                                  ident[:])
                    ins.then_inc(probs_turned, 1)

            def attend(t):
                for b in range(PAIR):
                    pe.wait_ge(probs_evac, PAIR * t + b + 1)
                    for q in range(2):
                        for k in range(q + 1):
                            n = k + q
                            ins = nc.tensor.matmul(att[b][:, q * EMB:(q + 1) * EMB],
                                                   probs_t[:, b, n * P:(n + 1) * P], ctx_rows[:, 2 * b + k],
                                                   start=(k == 0), stop=(k == q))
                    ins.then_inc(attended, 1)

            def gate_and_up(t, chunks, dt):
                for c in chunks:
                    if c == 0:
                        pe.wait_ge(xn_split, PAIR * (t + 1))
                    elif c in (1, 2):
                        pe.wait_ge(down_free, ROWS * t + 2 * c)
                    else:
                        pe.wait_ge(gated, HC * t + c - 2)
                    for which, done in ((0, gate_mm), (1, up_mm)):
                        bank = ring[(2 * c + which) % RING]
                        for k in range(EC):
                            at = ((c % 2 * 2 + which) * EC + k) * P
                            w = weights[:, c // 2, at:at + P].bitcast(dt)
                            for part in (xn_hi, xn_lo):
                                ins = nc.tensor.matmul(bank[:], w, part[:, k].bitcast(dt),
                                                       start=(k == 0 and part is xn_hi),
                                                       stop=(k == EC - 1 and part is xn_lo))
                        ins.then_inc(done, 1)

            def hidden(t, layer, chunks, dt):
                src = layer % 2
                for c in chunks:
                    if c == 0 and layer == 0:
                        pe.wait_ge(gated, HC * t + HC - 2)
                    elif c == 0:
                        pe.wait_ge(gelu_done, 2 * HC * t + HC - RING + 1)
                    elif c >= RING:
                        pe.wait_ge(gelu_done, 2 * HC * t + HC * layer + c - RING + 1)
                    bank = ring[(2 * HC + HC * layer + c) % RING]
                    for k in range(HC):
                        if c == 0:
                            pe.wait_ge(split, CH * t + HC * layer + k + 1)
                        w = weights[:, GU_P + H_P * layer + c, k * P:(k + 1) * P].bitcast(dt)
                        for part in (h_hi[src], h_lo[src]):
                            ins = nc.tensor.matmul(bank[:], w, part[:, k].bitcast(dt),
                                                   start=(k == 0 and part is h_hi[src]),
                                                   stop=(k == HC - 1 and part is h_lo[src]))
                    ins.then_inc(hid_mm, 1)

            def down(t, dt):
                for r in range(ROWS):
                    bank = ring[(4 * HC + r) % RING]
                    if r == 0:
                        pe.wait_ge(gelu_done, 2 * HC * t + 2 * HC - RING + 1)
                    for k in range(HC):
                        if r == 0:
                            pe.wait_ge(split, CH * t + 2 * HC + k + 1)
                        n, at = divmod(k * EMB, PIECE)
                        w = weights[:, GU_P + 2 * H_P + n, at:at + EMB].bitcast(dt)
                        for part in (h_hi[0], h_lo[0]):
                            ins = nc.tensor.matmul(bank[:, 0:EMB], part[:, k, r * P:(r + 1) * P].bitcast(dt), w,
                                                   start=(k == 0 and part is h_hi[0]),
                                                   stop=(k == HC - 1 and part is h_lo[0]))
                    ins.then_inc(down_mm, 1)

            def segment(seg, products):
                pe.wait_ge(flag_ready, seg + 1)
                flag = pe.value_load(seg_flags[0:1, seg:seg + 1].bitcast(I32), min_val=0, max_val=2**31 - 1)
                with pe.If(flag == 0):
                    products(F32R)
                with pe.Else():
                    products(F32)

            def tile(t, more=True):
                def hidden_segment(seg, layer, span):
                    segment(seg, lambda dt: hidden(t, layer, range(*span), dt))

                segment(GATE_UP_A, lambda dt: gate_and_up(t, range(HC // 2), dt))
                segment(GATE_UP_B, lambda dt: gate_and_up(t, range(HC // 2, HC), dt))
                hidden_segment(HID1A, 0, HID1_CHUNKS[HID1A])
                if more:
                    turn_rows(t + 1, 0, q_turned)
                hidden_segment(HID1B, 0, HID1_CHUNKS[HID1B])
                if more:
                    scores(t + 1)
                hidden_segment(HID2A, 1, HID2_CHUNKS[HID2A])
                if more:
                    turn_probs(t + 1)
                hidden_segment(HID2B, 1, HID2_CHUNKS[HID2B])
                if more:
                    attend(t + 1)
                hidden_segment(HID2C, 1, HID2_CHUNKS[HID2C])
                if more:
                    turn_rows(t + 1, 1, xn_turned)
                segment(DOWN, lambda dt: down(t, dt))

            pe.wait_ge(ident_made, 2)
            turn_rows(0, 0, q_turned)
            scores(0)
            turn_probs(0)
            attend(0)
            turn_rows(0, 1, xn_turned)
            with pe.Fori(0, TILES - 1) as t:
                tile(t)
            tile(TILES - 1, more=False)


def kernel(**inputs):
    import numpy as np
    import concourse.bacc as bacc
    from concourse.bass_utils import run_bass_kernel_spmd

    def chunked(w, chunks):
        w = np.asarray(w)
        return w.reshape(chunks, -1, w.shape[1] // P, P).transpose(0, 3, 2, 1)

    x = np.asarray(inputs["x"]).reshape(BATCH * SEQ, EMB)
    ctx = np.asarray(inputs["ctx_1024"])
    key_mask = np.asarray(inputs["mask_BxS2_ik1"])
    gate_up = np.stack([chunked(inputs["L0_ffn_w1_w"], HC), chunked(inputs["L0_ffn_w2_w"], HC)], axis=2)
    gate_up = gate_up.reshape(GU_P, 2, P, PIECE // 2).transpose(0, 2, 1, 3).reshape(GU_P, P, PIECE)
    hidden = [chunked(inputs[f"L0_ffn_h{n}_w"], HC).reshape(H_P, P, PIECE) for n in (1, 2)]
    down = chunked(inputs["L0_ffn_w3_w"], 1).reshape(P, DOWN_P, PIECE).transpose(1, 0, 2)
    scales = np.stack([np.asarray(inputs[f"L0_ffn_{n}_s"]).reshape(HC, P).T for n in ("w1", "w2", "h1", "h2")], axis=1)
    arrays = {
        "in_x": x,
        "in_ctx_rows": ctx.reshape(BATCH * SEQ, EMB),
        "in_ctx_cols": ctx.reshape(TILES, TOK, EC, P).transpose(0, 3, 2, 1),
        "in_mask": np.concatenate([key_mask[:, 0:P], key_mask], axis=1).reshape(TILES, PAIR * KEYS),
        "in_weights": np.concatenate([gate_up, *hidden, down]),
        "in_scales": scales,
        "in_down_scale": np.asarray(inputs["L0_ffn_w3_s"]),
    }
    arrays = {k: np.ascontiguousarray(a) for k, a in arrays.items()}
    nc = bacc.Bacc("TRN2", target_bir_lowering=False, num_devices=1)
    args = [nc.dram_tensor(k, a.shape, mybir.dt.from_np(a.dtype), kind="ExternalInput").ap() for k, a in arrays.items()]
    out = nc.dram_tensor("out_dram", (BATCH * SEQ, EMB), F32, kind="ExternalOutput").ap()
    xattn_ffn(nc, *args, out)
    results = run_bass_kernel_spmd(nc, [arrays], core_ids=[0])
    return results.results[0]["out_dram"].reshape(BATCH, SEQ, EMB)
```

```python
from contextlib import ExitStack

import concourse.bass as bass
from concourse import mybir

F32 = mybir.dt.float32
F32R = mybir.dt.float32r
BF16 = mybir.dt.bfloat16
I32 = mybir.dt.int32
U16 = mybir.dt.uint16
ALU = mybir.AluOpType
ACT = mybir.ActivationFunctionType
RADD = bass.bass_isa.ReduceOp.add

P = 128
BATCH, SEQ, EMB, HID = 8, 256, 256, 1024
PAIR = 2
TOK = PAIR * SEQ
TILES = BATCH // PAIR
ROWS = TOK // P
EC = EMB // P
HC = HID // P
KEYS = P + SEQ
EPS = 1e-5
SCALE = float(EMB) ** -0.5
MASKED = -1.5e38
FLOOR = -1.0e37

PIECE = 1024
GU_P = 2 * EC * HID // PIECE
H_P = HC * HID // PIECE
DOWN_P = HC * EMB // PIECE
PIECES = GU_P + 2 * H_P + DOWN_P
GATE_UP_A, GATE_UP_B, HID1A, HID1B, HID1C, HID2A, HID2B, HID2C, DOWN = range(9)
HID1_CHUNKS = {HID1A: (0, 3), HID1B: (3, 5), HID1C: (5, 8)}
HID2_CHUNKS = {HID2A: (0, 3), HID2B: (3, 5), HID2C: (5, 8)}
SPANS = {GATE_UP_A: (0, GU_P // 2), GATE_UP_B: (GU_P // 2, GU_P), DOWN: (PIECES - DOWN_P, PIECES)}
SPANS.update({seg: (GU_P + a, GU_P + b) for seg, (a, b) in HID1_CHUNKS.items()})
SPANS.update({seg: (GU_P + H_P + a, GU_P + H_P + b) for seg, (a, b) in HID2_CHUNKS.items()})
RING = 6
CH = 3 * HC


def xattn_ffn(nc, x, ctx_rows_d, ctx_cols_d, mask_d, weights_d, scales_d, down_scale_d, out):
    staged_d = nc.dram_tensor("weights_staged", [PIECES, P, PIECE], F32).ap()
    x_v = x.rearrange("(t r p) d -> t p r d", p=P, r=ROWS)
    ctx_v = ctx_rows_d.rearrange("(t r p) d -> t p r d", p=P, r=ROWS)
    out_v = out.rearrange("(t r p) d -> t p r d", p=P, r=ROWS)

    stack = ExitStack()
    with stack:
        def sb(name, shape, dt=F32):
            return stack.enter_context(nc.sbuf_tensor(name, shape, dt))

        def sem(name):
            return stack.enter_context(nc.semaphore(name))

        weights = sb("weights", [P, PIECES, PIECE], F32R)
        h_hi = [sb(f"h_hi{n}", [P, HC, TOK], F32R) for n in range(2)]
        h_lo = [sb(f"h_lo{n}", [P, HC, TOK], F32R) for n in range(2)]
        xn_hi = sb("xn_hi", [P, EC, TOK], F32R)
        xn_lo = sb("xn_lo", [P, EC, TOK], F32R)
        x_in = sb("x_in", [P, ROWS, EMB])
        x_attn = sb("x_attn", [P, ROWS, EMB])
        residual = sb("residual", [P, ROWS, EMB])
        ctx_rows = sb("ctx_rows", [P, ROWS, EMB])
        ctx_cols = sb("ctx_cols", [P, EC, TOK])
        mask = sb("mask", [P, PAIR, KEYS])
        work = sb("work", [P, ROWS * EMB])
        turned = sb("turned", [P, EC * TOK])
        gate = sb("gate", [P, 2, TOK])
        act32 = sb("act32", [P, 3, TOK])
        down_scale = sb("down_scale", [P, EMB])
        scales = sb("scales", [P, 4, HC])
        ident = sb("ident", [P, P])
        tri = sb("tri", [P, P])
        scaled = sb("scaled", [P, 2, EMB])
        low_sums = sb("low_sums", [P, PIECES])
        seg_flags = sb("seg_flags", [P, len(SPANS)])
        stats = sb("stats", [P, ROWS, 6])
        mean_var = sb("mean_var", [P, ROWS, 2])
        var_eps = sb("var_eps", [P, ROWS])
        rstd = sb("rstd", [P, ROWS])
        minus_half = sb("minus_half", [P, ROWS])
        row_max = sb("row_max", [P, ROWS])
        neg_max = sb("neg_max", [P, ROWS])
        row_sum = sb("row_sum", [P, ROWS])
        zero_col = sb("zero_col", [P, 1])
        table_out = sb("table_out", [P, 2])
        inv_sum = sb("inv_sum", [P, ROWS])

        xn = work[:].rearrange("p (r d) -> p r d", r=ROWS)
        probs = work[:, 0:PAIR * KEYS].rearrange("p (b k) -> p b k", b=PAIR)
        q_cols = turned[:].rearrange("p (b c t) -> p b c t", b=PAIR, c=EC)
        test_out = scaled[:].rearrange("p n d -> p (n d)").bitcast(BF16)
        probs_t = turned[:, 0:PAIR * KEYS].rearrange("p (b k) -> p b k", b=PAIR)
        gate_scale, up_scale, h1_scale, h2_scale = (scales[:, n] for n in range(4))

        att = [stack.enter_context(nc.psum_tensor(f"att{n}", [P, 512], F32)) for n in range(2)]
        ring = [stack.enter_context(nc.psum_tensor(f"ring{n}", [P, 512], F32)) for n in range(RING)]

        staged = [sem(f"staged{n}") for n in range(PIECES)]
        loaded = [sem(f"loaded{n}") for n in range(PIECES)]
        scales_in = sem("scales_in")
        down_scale_in = sem("down_scale_in")
        x_loaded = [sem(f"x_loaded{b}") for b in range(PAIR)]
        ctx_cols_in = sem("ctx_cols_in")
        ctx_rows_in = sem("ctx_rows_in")
        mask_loaded = sem("mask_loaded")
        out_stored = sem("out_stored")
        ident_made = sem("ident_made")
        idle_made = sem("idle_made")
        tri_made = sem("tri_made")
        pool_step = sem("pool_step")
        rstd_ready = sem("rstd_ready")
        flag_ready = sem("flag_ready")
        low_summed = sem("low_summed")
        q_evacuated = sem("q_evacuated")
        probs_ready = sem("probs_ready")
        xn_hi_ready = sem("xn_hi_ready")
        residual_set = sem("residual_set")
        gate_done = sem("gate_done")
        hi_done = sem("hi_done")
        gelu_done = sem("gelu_done")
        stats_step = sem("stats_step")
        moments = sem("moments")
        xn_ready = sem("xn_ready")
        maxed = sem("maxed")
        mask_step = sem("mask_step")
        mask_made = sem("mask_made")
        neg_ready = sem("neg_ready")
        inv_ready = sem("inv_ready")
        probs_evac = [sem(f"probs_evac{b}") for b in range(PAIR)]
        x_attn_done = sem("x_attn_done")
        xn_split = sem("xn_split")
        gated = sem("gated")
        hi_made = sem("hi_made")
        split = sem("split")
        down_free = sem("down_free")
        result_done = sem("result_done")
        q_turned = sem("q_turned")
        scores_done = sem("scores_done")
        probs_turned = sem("probs_turned")
        attended = sem("attended")
        xn_turned = sem("xn_turned")
        gate_mm = sem("gate_mm")
        up_mm = sem("up_mm")
        hid_mm = sem("hid_mm")
        down_mm = sem("down_mm")

        def key_cols(q):
            return slice(0, P) if q == 0 else slice(P, KEYS)

        block = stack.enter_context(nc.Block())

        @block.sync
        def _(sp):
            def load_queries(t):
                for b in range(PAIR):
                    rows = slice(2 * b, 2 * b + 2)
                    sp.dma_start(x_in[:, rows], x_v[t][:, rows]).then_inc(x_loaded[b], 16)

            def load_keys(t):
                sp.dma_start(ctx_cols[:], ctx_cols_d[t]).then_inc(ctx_cols_in, 16)

            def load_mask(t):
                sp.dma_start(mask[:].bitcast(I32), mask_d[t].partition_broadcast(P)).then_inc(mask_loaded, 16)

            def load_values(t):
                sp.dma_start(ctx_rows[:], ctx_v[t]).then_inc(ctx_rows_in, 16)

            def load_next(t):
                sp.wait_ge(x_attn_done, ROWS * t)
                load_queries(t)
                load_keys(t)
                load_mask(t)
                load_values(t)

            def stage(n):
                sp.dma_start(staged_d[n], weights_d[n]).then_inc(staged[n], 16)

            def load_piece(n):
                sp.wait_ge(staged[n], 16)
                sp.dma_start(weights[:, n].bitcast(F32), staged_d[n]).then_inc(loaded[n], 16)

            def store(t):
                for r in range(ROWS):
                    sp.wait_ge(result_done, ROWS * t + r + 1)
                    sp.dma_start(out_v[t][:, r], residual[:, r]).then_inc(out_stored, 16)

            load_queries(0)
            load_keys(0)
            load_mask(0)
            stage(0)
            stage(1)
            load_values(0)
            load_piece(0)
            sp.dma_start(scales[:], scales_d).then_inc(scales_in, 16)
            load_piece(1)
            ahead = 2
            for n in range(2, 2 + ahead):
                stage(n)
            for n in range(2, PIECES):
                load_piece(n)
                if n + ahead < PIECES:
                    stage(n + ahead)
                if n == SPANS[HID1A][0]:
                    sp.dma_start(down_scale[:], down_scale_d.partition_broadcast(P)).then_inc(down_scale_in, 16)
                if n == SPANS[HID1B][0]:
                    sp.wait_ge(x_attn_done, ROWS)
                    load_queries(1)
                if n == SPANS[HID1C][1] - 1:
                    load_keys(1)
                    load_mask(1)
                    load_values(1)
            with sp.Fori(0, TILES - 2) as t:
                load_next(t + 2)
                store(t)
            for t in range(TILES - 2, TILES):
                store(t)
            sp.wait_ge(out_stored, 16 * ROWS * TILES)

        @block.gpsimd
        def _(pool):
            steps = [0]

            def chain(ins):
                ins.then_inc(pool_step, 1)
                steps[0] += 1
                pool.wait_ge(pool_step, steps[0])

            chain(nc.gpsimd.memset(ident[:], 0.0))
            nc.gpsimd.affine_select(out=ident[:], in_=ident[:], compare_op=ALU.not_equal, fill=1.0, base=0,
                                    pattern=[[-1, P]], channel_multiplier=1).then_inc(ident_made, 1)
            nc.gpsimd.memset(minus_half[:], -0.5).then_inc(ident_made, 1)
            chain(nc.gpsimd.memset(tri[:], 0.0))
            nc.gpsimd.affine_select(out=tri[:], in_=tri[:], compare_op=ALU.is_ge, fill=MASKED, base=0,
                                    pattern=[[-1, P]], channel_multiplier=1).then_inc(tri_made, 1)
            pool.wait_ge(ident_made, 2)

            def make_rstd(t, norm, rows=range(ROWS)):
                pool.wait_ge(moments, ROWS * (2 * t + norm) + rows[-1] + 1)
                cols = slice(rows[0], rows[-1] + 1)
                chain(nc.gpsimd.tensor_scalar(var_eps[:, cols], mean_var[:, cols, 1], 1.0, EPS, ALU.mult, ALU.add))
                nc.gpsimd.tensor_tensor(rstd[:, cols], var_eps[:, cols], minus_half[:, cols], op=ALU.pow
                                        ).then_inc(rstd_ready, len(rows))

            def combine_flag(seg):
                first, end = SPANS[seg]
                pool.wait_ge(low_summed, end)
                while end - first > 1:
                    h = (end - first) // 2
                    chain(nc.gpsimd.tensor_tensor(low_sums[:, first:first + h], low_sums[:, first:first + h],
                                                  low_sums[:, end - h:end], op=ALU.add))
                    end -= h
                nc.gpsimd.partition_all_reduce(seg_flags[:, seg:seg + 1], low_sums[:, first:first + 1], P, RADD
                                               ).then_inc(flag_ready, 1)

            make_rstd(0, 0, range(0, 2))
            make_rstd(0, 0, range(2, ROWS))
            make_rstd(0, 1, range(0, 2))
            combine_flag(GATE_UP_A)
            make_rstd(0, 1, range(2, ROWS))
            combine_flag(GATE_UP_B)
            combine_flag(HID1A)
            combine_flag(HID1B)
            make_rstd(1, 0)
            for seg in (HID1C, HID2A, HID2B, HID2C):
                combine_flag(seg)
            make_rstd(1, 1)
            combine_flag(DOWN)
            for t in range(2, TILES):
                make_rstd(t, 0)
                make_rstd(t, 1)

        @block.scalar
        def _(act):
            def test_piece(n):
                act.wait_ge(loaded[n], 16)
                if n:
                    act.wait_ge(low_summed, n)
                low = weights[:, n].bitcast(U16)[:, 0:2 * PIECE:2]
                nc.scalar.activation(test_out, low, ACT.Copy, accum_out=low_sums[:, n:n + 1]
                                     ).then_inc(low_summed, 1)

            def evacuate_q(t):
                for b in range(PAIR):
                    act.wait_ge(q_turned, PAIR * t + b + 1)
                    nc.scalar.activation(turned[:, b * 512:(b + 1) * 512], att[b][:], ACT.Copy, scale=SCALE
                                         ).then_inc(q_evacuated, 1)

            def exponentials(t):
                for n in range(ROWS):
                    b, cols = n // 2, key_cols(n % 2)
                    if n % 2 == 0:
                        act.wait_ge(neg_ready, PAIR * t + b + 1)
                    nc.scalar.activation(probs[:, b, cols], probs[:, b, cols], ACT.Exp, bias=neg_max[:, n:n + 1],
                                         accum_out=row_sum[:, n:n + 1]).then_inc(probs_ready, 1)

            def split_xn(t):
                for b in range(PAIR):
                    act.wait_ge(xn_turned, PAIR * t + b + 1)
                    nc.scalar.activation(xn_hi[:, :, b * SEQ:(b + 1) * SEQ],
                                         att[b][:].rearrange("p (c t) -> p c t", c=EC), ACT.Copy
                                         ).then_inc(xn_hi_ready, 1)

            def set_residual(t):
                act.wait_ge(x_attn_done, ROWS * (t + 1))
                if not isinstance(t, int) or t > 0:
                    act.wait_ge(out_stored, 16 * ROWS * t)
                nc.scalar.activation(residual[:], x_attn[:], ACT.Copy).then_inc(residual_set, 1)

            def hi_part(t, c):
                act.wait_ge(gated, HC * t + c + 1)
                nc.scalar.activation(h_hi[0][:, c], act32[:, c % 3], ACT.Copy).then_inc(hi_done, 1)

            def first_layer(t, tests=()):
                for c in range(HC + 1):
                    if c < HC:
                        act.wait_ge(gate_mm, HC * t + c + 1)
                        if c >= 2 or not isinstance(t, int) or t > 0:
                            act.wait_ge(gated, HC * t + c - 1)
                        nc.scalar.activation(gate[:, c % 2], ring[2 * c % RING][:], ACT.Silu,
                                             scale=gate_scale[:, c:c + 1]).then_inc(gate_done, 1)
                    if c >= 1:
                        hi_part(t, c - 1)
                    if c in (0, 2, 4) and tests:
                        test_piece(tests.pop(0))

            def gelu(t, layer, c):
                n = HC * (layer + 1) + c
                scale = (h1_scale, h2_scale)[layer]
                act.wait_ge(hid_mm, 2 * HC * t + HC * layer + c + 1)
                act.wait_ge(split, CH * t + n - 2)
                nc.scalar.activation(act32[:, n % 3], ring[(2 * HC + HC * layer + c) % RING][:], ACT.Gelu,
                                     scale=scale[:, c:c + 1]).then_inc(gelu_done, 1)

            def tile(t, tests=None, more=True):
                tests = tests or {}
                first_layer(t, tests.get("first layer", []))
                for layer in range(2):
                    for c in range(HC):
                        gelu(t, layer, c)
                        if (layer, c) == (0, 1):
                            set_residual(t)
                        for n in tests.get((layer, c), []):
                            test_piece(n)
                        if more and (layer, c) == (0, HID1_CHUNKS[HID1B][1] - 1):
                            evacuate_q(t + 1)
                        if more and (layer, c) == (0, HC - 1):
                            exponentials(t + 1)
                if more:
                    split_xn(t + 1)
                    load_table(1, ACT.Silu)

            def load_table(n, function):
                nc.scalar.activation(table_out[:, n:n + 1], zero_col[:], function)

            act.wait_ge(down_free, ROWS)
            load_table(0, ACT.Exp)
            evacuate_q(0)
            exponentials(0)
            act.wait_ge(probs_turned, PAIR)
            nc.scalar.activation(probs_t[:, 1], att[1][:, 0:KEYS], ACT.Copy).then_inc(probs_evac[1], 1)
            load_table(1, ACT.Silu)
            for n in range(*SPANS[GATE_UP_A]):
                test_piece(n)
            split_xn(0)
            for n in range(*SPANS[GATE_UP_B]):
                test_piece(n)
            act.wait_ge(scales_in, 16)
            tests = {"first layer": list(range(*SPANS[HID1A]))}
            after = ((0, 0), (0, 0), (0, 1), (0, 1), (0, 2), (0, 4), (0, 5), (0, 6),
                     (1, 0), (1, 1), (1, 2), (1, 3), (1, 3), (1, 5), (1, 6))
            for n, at in zip(range(SPANS[HID1B][0], PIECES), after, strict=True):
                tests.setdefault(at, []).append(n)
            tile(0, tests)
            with act.Fori(1, TILES - 1) as t:
                tile(t)
            tile(TILES - 1, more=False)

        @block.vector
        def _(dve):
            def norm_stats(r, src):
                nc.vector.bn_stats(out=stats[:, r], in_=src[:, r]).then_inc(stats_step, 1)

            def wait_stats(t, norm, r):
                dve.wait_ge(stats_step, ROWS * (2 * t + norm) + r + 1)

            def norm_moments(r):
                nc.vector.bn_aggr(out=mean_var[:, r], in_=stats[:, r]).then_inc(moments, 1)

            def normalise(t, norm, src, r):
                if r % 2 == 0:
                    dve.wait_ge(moments, ROWS * (2 * t + norm) + r + 2)
                    dve.wait_ge(rstd_ready, ROWS * (2 * t + norm) + (r + 2 if isinstance(t, int) and t == 0 else ROWS))
                nc.vector.tensor_scalar(xn[:, r], src[:, r], mean_var[:, r, 0:1], rstd[:, r:r + 1],
                                        ALU.subtract, ALU.mult).then_inc(xn_ready, 1)

            def make_mask(t):
                dve.wait_ge(mask_loaded, 16 * (t + 1))
                nc.vector.tensor_scalar(mask[:], mask[:].bitcast(I32), 0.0, MASKED, ALU.is_equal, ALU.mult
                                        ).then_inc(mask_step, 1)
                dve.wait_ge(mask_step, t + 1)
                for b in range(PAIR):
                    for at in (0, KEYS - P):
                        ins = nc.vector.tensor_tensor(mask[:, b, at:at + P], mask[:, b, at:at + P], tri[:],
                                                      op=ALU.add)
                ins.then_inc(mask_made, 1)

            def wait_scores(t):
                dve.wait_ge(mask_made, t + 1)
                dve.wait_ge(scores_done, PAIR * (t + 1))

            def mask_and_max(t, b):
                for n in (2 * b, 2 * b + 1):
                    cols = key_cols(n % 2)
                    nc.vector.tensor_tensor_reduce(out=probs[:, b, cols], in0=att[b][:, cols], in1=mask[:, b, cols],
                                                   scale=1.0, scalar=FLOOR, op0=ALU.add, op1=ALU.max,
                                                   accum_out=row_max[:, n:n + 1]).then_inc(maxed, 1)
                dve.wait_ge(maxed, ROWS * t + 2 * b + 2)
                nc.vector.tensor_scalar(neg_max[:, 2 * b:2 * b + 2], row_max[:, 2 * b:2 * b + 2], -1.0, None, ALU.mult
                                        ).then_inc(neg_ready, 1)

            def evacuate_probs(t, b):
                dve.wait_ge(probs_turned, PAIR * t + b + 1)
                nc.vector.tensor_copy(probs_t[:, b], att[b][:, 0:KEYS]).then_inc(probs_evac[b], 1)

            def add_attention(t, b):
                if b == 0:
                    dve.wait_ge(probs_ready, ROWS * (t + 1))
                    nc.vector.reciprocal(inv_sum[:], row_sum[:]).then_inc(inv_ready, 1)
                    dve.wait_ge(inv_ready, t + 1)
                if b == 0 and (not isinstance(t, int) or t > 0):
                    dve.wait_ge(residual_set, t)
                dve.wait_ge(attended, PAIR * t + b + 1)
                for r in (2 * b, 2 * b + 1):
                    nc.vector.scalar_tensor_tensor(out=x_attn[:, r], in0=att[b][:, (r % 2) * EMB:][:, 0:EMB],
                                                   scalar=inv_sum[:, r:r + 1], in1=x_in[:, r],
                                                   op0=ALU.mult, op1=ALU.add).then_inc(x_attn_done, 1)

            def stats_after_attention(t, b):
                for r in (2 * b, 2 * b + 1):
                    dve.wait_ge(x_attn_done, ROWS * t + r + 1)
                    norm_stats(r, x_attn)

            def moments_after_attention(t, b):
                for r in (2 * b, 2 * b + 1):
                    wait_stats(t, 1, r)
                    norm_moments(r)

            def split_xn(t, b):
                toks = slice(b * SEQ, (b + 1) * SEQ)
                dve.wait_ge(xn_hi_ready, PAIR * t + b + 1)
                nc.vector.tensor_tensor(xn_lo[:, :, toks], att[b][:].rearrange("p (c t) -> p c t", c=EC),
                                        xn_hi[:, :, toks].bitcast(F32), op=ALU.subtract).then_inc(xn_split, 1)

            def lo_part(t, n, buf, c):
                nc.vector.tensor_tensor(h_lo[buf][:, c], act32[:, n % 3], h_hi[buf][:, c].bitcast(F32),
                                        op=ALU.subtract).then_inc(split, 1)

            def first_layer(t):
                for c in range(HC + 1):
                    if c < HC:
                        dve.wait_ge(up_mm, HC * t + c + 1)
                        dve.wait_ge(gate_done, HC * t + c + 1)
                        if not isinstance(t, int) or CH * t + c - 2 > 0:
                            dve.wait_ge(split, CH * t + c - 2)
                        nc.vector.scalar_tensor_tensor(out=act32[:, c % 3], in0=ring[(2 * c + 1) % RING][:],
                                                       scalar=up_scale[:, c:c + 1], in1=gate[:, c % 2],
                                                       op0=ALU.mult, op1=ALU.mult).then_inc(gated, 1)
                    if c >= 1:
                        dve.wait_ge(hi_done, HC * t + c)
                        lo_part(t, c - 1, 0, c - 1)

            def split_hidden(t, layer, c):
                n = HC * (layer + 1) + c
                buf = (layer + 1) % 2
                dve.wait_ge(gelu_done, 2 * HC * t + HC * layer + c + 1)
                nc.vector.tensor_copy(h_hi[buf][:, c], act32[:, n % 3]).then_inc(hi_made, 1)
                dve.wait_ge(hi_made, 2 * HC * t + HC * layer + c + 1)
                lo_part(t, n, buf, c)

            def results(t):
                dve.wait_ge(down_scale_in, 16)
                dve.wait_ge(residual_set, t + 1)
                for r in range(ROWS):
                    bank = ring[(4 * HC + r) % RING]
                    dve.wait_ge(down_mm, ROWS * t + r + 1)
                    if r >= 2:
                        dve.wait_ge(result_done, ROWS * t + r - 1)
                    nc.vector.tensor_tensor(scaled[:, r % 2], bank[:, 0:EMB], down_scale[:], op=ALU.mult
                                            ).then_inc(down_free, 1)
                    dve.wait_ge(down_free, ROWS * (t + 1) + r + 1)
                    nc.vector.tensor_tensor(residual[:, r], residual[:, r], scaled[:, r % 2], op=ALU.add
                                            ).then_inc(result_done, 1)

            def tile(t, more=True):
                first_layer(t)
                for layer in range(2):
                    for c in range(HC):
                        at = (layer, c) if more else None
                        if at == (0, 1):
                            wait_stats(t + 1, 0, ROWS - 1)
                        if at == (0, HC - 1):
                            wait_scores(t + 1)
                        if at == (1, HID2_CHUNKS[HID2C][0]):
                            wait_stats(t + 1, 1, ROWS - 1)
                        split_hidden(t, layer, c)
                        if at == (0, 0):
                            for r in range(ROWS):
                                if r % 2 == 0:
                                    dve.wait_ge(x_loaded[r // 2], 16 * (t + 2))
                                norm_stats(r, x_in)
                        if at in ((0, 1), (1, HID2_CHUNKS[HID2C][0])):
                            for r in range(ROWS):
                                norm_moments(r)
                        if at == (0, 2):
                            for r in range(ROWS):
                                normalise(t + 1, 0, x_in, r)
                        if at == (0, 4):
                            make_mask(t + 1)
                        if at == (0, HC - 1):
                            for b in range(PAIR):
                                mask_and_max(t + 1, b)
                        if at == (1, HID2_CHUNKS[HID2A][1] - 1):
                            for b in range(PAIR):
                                evacuate_probs(t + 1, b)
                        if at == (1, HID2_CHUNKS[HID2B][1] - 1):
                            for b in range(PAIR):
                                add_attention(t + 1, b)
                                stats_after_attention(t + 1, b)
                        if at == (1, HID2_CHUNKS[HID2C][0] + 1):
                            for r in range(ROWS):
                                normalise(t + 1, 1, x_attn, r)
                if more:
                    for b in range(PAIR):
                        split_xn(t + 1, b)
                results(t)

            nc.vector.memset(zero_col[:], 0.0).then_inc(down_free, ROWS)
            nc.vector.memset(h_lo[0][:, 0].bitcast(F32), 0.0).then_inc(idle_made, 1)
            for b in range(PAIR):
                dve.wait_ge(x_loaded[b], 16)
                for r in (2 * b, 2 * b + 1):
                    norm_stats(r, x_in)
                for r in (2 * b, 2 * b + 1):
                    wait_stats(0, 0, r)
                    norm_moments(r)
            for r in range(ROWS):
                normalise(0, 0, x_in, r)
            dve.wait_ge(tri_made, 1)
            make_mask(0)
            dve.wait_ge(mask_made, 1)
            for b in range(PAIR):
                dve.wait_ge(scores_done, b + 1)
                mask_and_max(0, b)
            evacuate_probs(0, 0)
            for b in range(PAIR):
                add_attention(0, b)
                stats_after_attention(0, b)
                moments_after_attention(0, b)
            for r in range(ROWS):
                normalise(0, 1, x_attn, r)
            for b in range(PAIR):
                split_xn(0, b)
            dve.wait_ge(scales_in, 16)
            tile(0)
            with dve.Fori(1, TILES - 1) as t:
                tile(t)
            tile(TILES - 1, more=False)

        @block.tensor
        def _(pe):
            def turn_rows(t, norm, done):
                for b in range(PAIR):
                    for r in (2 * b, 2 * b + 1):
                        pe.wait_ge(xn_ready, ROWS * (2 * t + norm) + r + 1)
                        for c in range(EC):
                            at = c * SEQ + r % 2 * P
                            ins = nc.tensor.transpose(att[b][:, at:at + P], xn[:, r, c * P:(c + 1) * P], ident[:])
                    ins.then_inc(done, 1)

            def scores(t):
                pe.wait_ge(ctx_cols_in, 16 * (t + 1))
                for b in range(PAIR):
                    pe.wait_ge(q_evacuated, PAIR * t + b + 1)
                    for q in range(2):
                        cols = key_cols(q)
                        for c in range(EC):
                            ins = nc.tensor.matmul(att[b][:, cols], q_cols[:, b, c, q * P:(q + 1) * P],
                                                   ctx_cols[:, c, b * SEQ:b * SEQ + (q + 1) * P],
                                                   start=(c == 0), stop=(c == EC - 1))
                    ins.then_inc(scores_done, 1)

            def turn_probs(t, b):
                pe.wait_ge(probs_ready, ROWS * t + 2 * b + 2)
                for n in range(KEYS // P):
                    ins = nc.tensor.transpose(att[b][:, n * P:(n + 1) * P], probs[:, b, n * P:(n + 1) * P],
                                              ident[:])
                ins.then_inc(probs_turned, 1)

            def attend(t, b):
                if b == 0:
                    pe.wait_ge(ctx_rows_in, 16 * (t + 1))
                pe.wait_ge(probs_evac[b], t + 1)
                for q in range(2):
                    for k in range(q + 1):
                        n = k + q
                        ins = nc.tensor.matmul(att[b][:, q * EMB:(q + 1) * EMB],
                                               probs_t[:, b, n * P:(n + 1) * P], ctx_rows[:, 2 * b + k],
                                               start=(k == 0), stop=(k == q))
                ins.then_inc(attended, 1)

            def gate_and_up(t, chunks, dt):
                ahead = [c for c in chunks if c < RING // 2]
                order = [(c, b, slice(b * SEQ, (b + 1) * SEQ)) for b in range(PAIR) for c in ahead]
                order += [(c, None, slice(0, TOK)) for c in chunks if c not in ahead]
                for c, b, toks in order:
                    if c == 0:
                        pe.wait_ge(xn_split, PAIR * t + b + 1)
                    elif c in ahead and b == 0:
                        pe.wait_ge(down_free, ROWS * t + 2 * c)
                    elif b is None:
                        pe.wait_ge(gated, HC * t + c - 2)
                    for which, done in ((0, gate_mm), (1, up_mm)):
                        bank = ring[(2 * c + which) % RING]
                        for k in range(EC):
                            at = ((c % 2 * 2 + which) * EC + k) * P
                            w = weights[:, c // 2, at:at + P].bitcast(dt)
                            for part in (xn_hi, xn_lo):
                                ins = nc.tensor.matmul(bank[:, toks], w, part[:, k, toks].bitcast(dt),
                                                       start=(k == 0 and part is xn_hi),
                                                       stop=(k == EC - 1 and part is xn_lo))
                        if toks.stop == TOK:
                            ins.then_inc(done, 1)

            def hidden(t, layer, chunks, dt):
                src = layer % 2
                for c in chunks:
                    if c == 0 and layer == 0:
                        pe.wait_ge(gated, HC * t + HC - 2)
                    elif c == 0:
                        pe.wait_ge(gelu_done, 2 * HC * t + HC - RING + 1)
                    elif c >= RING:
                        pe.wait_ge(gelu_done, 2 * HC * t + HC * layer + c - RING + 1)
                    bank = ring[(2 * HC + HC * layer + c) % RING]
                    for k in range(HC):
                        if c == 0:
                            pe.wait_ge(split, CH * t + HC * layer + k + 1)
                        w = weights[:, GU_P + H_P * layer + c, k * P:(k + 1) * P].bitcast(dt)
                        for part in (h_hi[src], h_lo[src]):
                            ins = nc.tensor.matmul(bank[:], w, part[:, k].bitcast(dt),
                                                   start=(k == 0 and part is h_hi[src]),
                                                   stop=(k == HC - 1 and part is h_lo[src]))
                    ins.then_inc(hid_mm, 1)

            def down(t, dt):
                last = HC - 1
                for r, chunks in ((0, range(last)), (1, range(last)), (0, (last,)), (1, (last,)),
                                  (2, range(HC)), (3, range(HC))):
                    bank = ring[(4 * HC + r) % RING]
                    if r < 2 and chunks[0] == 0:
                        pe.wait_ge(gelu_done, 2 * HC * t + 2 * HC - RING + 1 + r)
                    for k in chunks:
                        if r == 0:
                            pe.wait_ge(split, CH * t + 2 * HC + k + 1)
                        n, at = divmod(k * EMB, PIECE)
                        w = weights[:, GU_P + 2 * H_P + n, at:at + EMB].bitcast(dt)
                        for part in (h_hi[0], h_lo[0]):
                            ins = nc.tensor.matmul(bank[:, 0:EMB], part[:, k, r * P:(r + 1) * P].bitcast(dt), w,
                                                   start=(k == 0 and part is h_hi[0]),
                                                   stop=(k == last and part is h_lo[0]))
                    if chunks[-1] == last:
                        ins.then_inc(down_mm, 1)

            def segment(seg, products):
                pe.wait_ge(flag_ready, seg + 1)
                flag = pe.value_load(seg_flags[0:1, seg:seg + 1].bitcast(I32), min_val=0, max_val=2**31 - 1)
                with pe.If(flag == 0):
                    products(F32R)
                with pe.Else():
                    products(F32)

            def tile(t, more=True):
                def hidden_segment(seg, layer, span):
                    segment(seg, lambda dt: hidden(t, layer, range(*span), dt))

                segment(GATE_UP_A, lambda dt: gate_and_up(t, range(HC // 2), dt))
                segment(GATE_UP_B, lambda dt: gate_and_up(t, range(HC // 2, HC), dt))
                hidden_segment(HID1A, 0, HID1_CHUNKS[HID1A])
                hidden_segment(HID1B, 0, HID1_CHUNKS[HID1B])
                if more:
                    turn_rows(t + 1, 0, q_turned)
                hidden_segment(HID1C, 0, HID1_CHUNKS[HID1C])
                if more:
                    scores(t + 1)
                hidden_segment(HID2A, 1, HID2_CHUNKS[HID2A])
                if more:
                    for b in range(PAIR):
                        turn_probs(t + 1, b)
                hidden_segment(HID2B, 1, HID2_CHUNKS[HID2B])
                if more:
                    for b in range(PAIR):
                        attend(t + 1, b)
                hidden_segment(HID2C, 1, HID2_CHUNKS[HID2C])
                if more:
                    turn_rows(t + 1, 1, xn_turned)
                segment(DOWN, lambda dt: down(t, dt))

            def stay_busy(n):
                for _ in range(n):
                    nc.tensor.matmul(ring[RING - 1][:], h_lo[0][:, 0, 0:P], h_lo[0][:, 0], start=True, stop=True)

            pe.wait_ge(idle_made, 1)
            stay_busy(10)
            pe.wait_ge(ident_made, 2)
            turn_rows(0, 0, q_turned)
            scores(0)
            stay_busy(2)
            turn_probs(0, 0)
            stay_busy(1)
            turn_probs(0, 1)
            for b in range(PAIR):
                attend(0, b)
            stay_busy(13)
            turn_rows(0, 1, xn_turned)
            stay_busy(2)
            with pe.Fori(0, TILES - 1) as t:
                tile(t)
            tile(TILES - 1, more=False)


def kernel(**inputs):
    import numpy as np
    import concourse.bacc as bacc
    from concourse.bass_utils import run_bass_kernel_spmd

    def chunked(w, chunks):
        w = np.asarray(w)
        return w.reshape(chunks, -1, w.shape[1] // P, P).transpose(0, 3, 2, 1)

    x = np.asarray(inputs["x"]).reshape(BATCH * SEQ, EMB)
    ctx = np.asarray(inputs["ctx_1024"])
    key_mask = np.asarray(inputs["mask_BxS2_ik1"])
    gate_up = np.stack([chunked(inputs["L0_ffn_w1_w"], HC), chunked(inputs["L0_ffn_w2_w"], HC)], axis=2)
    gate_up = gate_up.reshape(GU_P, 2, P, PIECE // 2).transpose(0, 2, 1, 3).reshape(GU_P, P, PIECE)
    hidden = [chunked(inputs[f"L0_ffn_h{n}_w"], HC).reshape(H_P, P, PIECE) for n in (1, 2)]
    down = chunked(inputs["L0_ffn_w3_w"], 1).reshape(P, DOWN_P, PIECE).transpose(1, 0, 2)
    scales = np.stack([np.asarray(inputs[f"L0_ffn_{n}_s"]).reshape(HC, P).T for n in ("w1", "w2", "h1", "h2")], axis=1)
    arrays = {
        "in_x": x,
        "in_ctx_rows": ctx.reshape(BATCH * SEQ, EMB),
        "in_ctx_cols": ctx.reshape(TILES, TOK, EC, P).transpose(0, 3, 2, 1),
        "in_mask": np.concatenate([key_mask[:, 0:P], key_mask], axis=1).reshape(TILES, PAIR * KEYS),
        "in_weights": np.concatenate([gate_up, *hidden, down]),
        "in_scales": scales,
        "in_down_scale": np.asarray(inputs["L0_ffn_w3_s"]),
    }
    arrays = {k: np.ascontiguousarray(a) for k, a in arrays.items()}
    nc = bacc.Bacc("TRN2", target_bir_lowering=False, num_devices=1)
    args = [nc.dram_tensor(k, a.shape, mybir.dt.from_np(a.dtype), kind="ExternalInput").ap() for k, a in arrays.items()]
    out = nc.dram_tensor("out_dram", (BATCH * SEQ, EMB), F32, kind="ExternalOutput").ap()
    xattn_ffn(nc, *args, out)
    results = run_bass_kernel_spmd(nc, [arrays], core_ids=[0])
    return results.results[0]["out_dram"].reshape(BATCH, SEQ, EMB)
```
